# Optimizing a Trainium2 kernel written in Bass

```python
import numpy as np
import jax
import jax.numpy as jnp

def _softmax(x, axis=-1):
    return jax.nn.softmax(x, axis=axis)

def _gelu(x):
    return jax.nn.gelu(x, approximate=True)

def _silu(x):
    return jax.nn.silu(x)

def _sigmoid(x):
    return jax.nn.sigmoid(x)

def _layernorm(x, axis=-1, eps=1e-05):
    m = jnp.mean(x, axis=axis, keepdims=True)
    v = jnp.var(x, axis=axis, keepdims=True)
    return (x - m) / jnp.sqrt(v + eps)

def _scatter_add(tgt, idx, src, axis=0):
    return tgt.at[idx].add(src)

def _segment_sum(src, seg, n):
    return jax.ops.segment_sum(src, seg, n)
kernel_name = 'mk_adj_preln_d4_adj_r2_ec4d1a'

def setup_inputs(seed: int=0):
    np.random.seed(seed)
    _w = jnp.asarray

    def _rec_inputs():
        import jax
        import jax.numpy as jnp
        _gk = jax.random.key(seed)
        x = -0.0002928 + 1 * jax.random.normal(jax.random.fold_in(_gk, 1), (8, 1024, 128), jnp.float32)
        _a = jax.random.bernoulli(jax.random.fold_in(_gk, 2), 0.00195312, (8, 1024, 1024))
        adj = _a.astype(jnp.int32)
        _nm = jnp.ones((8, 1024), dtype=bool)
        nodemask = jnp.where(_nm, 1.0, 0.0).astype(jnp.float32)
        return (x, adj, nodemask)
    x, adj, nodemask = _rec_inputs()

    def _L0_gnn_setup():
        import jax, jax.numpy as jnp
        import numpy as np
        OUT = 128
        NUM_LAYERS = 3

        def _gru_cell(inp, h, w_ih, w_hh, b_ih, b_hh):
            gi = inp @ w_ih.T + b_ih
            gh = h @ w_hh.T + b_hh
            i_r, i_z, i_n = jnp.split(gi, 3, axis=-1)
            h_r, h_z, h_n = jnp.split(gh, 3, axis=-1)
            r = jax.nn.sigmoid(i_r + h_r)
            z = jax.nn.sigmoid(i_z + h_z)
            n = jnp.tanh(i_n + r * h_n)
            return (1.0 - z) * n + z * h
        key = jax.random.key(seed)
        ks = jax.random.split(key, 8)
        B, N, D = (32, 256, 128)
        x = jax.random.normal(ks[0], (B, N, D), dtype=jnp.float32)
        adj = jax.random.randint(ks[1], (B, N, N), 0, 2, dtype=jnp.int32)
        s = 1.0 / np.sqrt(OUT)
        weight = jax.random.uniform(ks[2], (NUM_LAYERS, OUT, OUT), jnp.float32, -s, s)
        w_ih = jax.random.uniform(ks[3], (3 * OUT, OUT), jnp.float32, -s, s)
        w_hh = jax.random.uniform(ks[4], (3 * OUT, OUT), jnp.float32, -s, s)
        b_ih = jax.random.uniform(ks[5], (3 * OUT,), jnp.float32, -s, s)
        b_hh = jax.random.uniform(ks[6], (3 * OUT,), jnp.float32, -s, s)
        return {'x': x, 'adj': adj, 'weight': weight, 'w_ih': w_ih, 'w_hh': w_hh, 'b_ih': b_ih, 'b_hh': b_hh}
    _L0_gnn_all = _L0_gnn_setup()
    _L0_gnn_in = {k: v for k, v in _L0_gnn_all.items() if k in ('weight', 'w_ih', 'w_hh', 'b_ih', 'b_hh')}
    del _L0_gnn_all

    def _L1_gnn_setup():
        import jax, jax.numpy as jnp
        import numpy as np
        UNITS = 128
        NUM_HEADS = 8
        HEAD_DIM = UNITS // NUM_HEADS
        B, N = (8, 1024)
        key = jax.random.key(seed)
        ks = jax.random.split(key, 7)
        node_features = jax.random.normal(ks[0], (B, N, UNITS), dtype=jnp.float32)
        adjacency_matrix = jax.random.randint(ks[1], (B, N, N), 0, 2, dtype=jnp.int32)
        s = 1.0 / np.sqrt(UNITS)
        Wq = jax.random.normal(ks[2], (UNITS, UNITS), dtype=jnp.float32) * s
        Wk = jax.random.normal(ks[3], (UNITS, UNITS), dtype=jnp.float32) * s
        Wv = jax.random.normal(ks[4], (UNITS, UNITS), dtype=jnp.float32) * s
        Wo = jax.random.normal(ks[5], (UNITS, UNITS), dtype=jnp.float32) * s
        bo = jnp.zeros((UNITS,), dtype=jnp.float32)
        return {'node_features': node_features, 'adjacency_matrix': adjacency_matrix, 'Wq': Wq, 'Wk': Wk, 'Wv': Wv, 'Wo': Wo, 'bo': bo}
    _L1_gnn_all = _L1_gnn_setup()
    _L1_gnn_in = {k: v for k, v in _L1_gnn_all.items() if k in ('Wq', 'Wk', 'Wv', 'Wo', 'bo')}
    del _L1_gnn_all

    def _L2_gnn_setup():
        import jax, jax.numpy as jnp
        import numpy as np
        ALPHA = 0.2
        NEG_BIG = -9000000000000000.0
        key = jax.random.key(seed)
        k1, k2, k3, k4 = jax.random.split(key, 4)
        B, N, Fin, Fout = (16, 512, 128, 128)
        h = jax.random.normal(k1, (B, N, Fin), dtype=jnp.float32)
        adj = jax.random.randint(k2, (B, N, N), 0, 2, dtype=jnp.int32)
        mask = jnp.ones((B, N), dtype=jnp.float32)
        gain = 1.414
        limW = gain * np.sqrt(6.0 / (Fin + Fout))
        W = jax.random.uniform(k3, (Fin, Fout), minval=-limW, maxval=limW, dtype=jnp.float32)
        lima = gain * np.sqrt(6.0 / (2 * Fout + 1))
        a = jax.random.uniform(k4, (2 * Fout, 1), minval=-lima, maxval=lima, dtype=jnp.float32)
        return {'h': h, 'adj': adj, 'mask': mask, 'W': W, 'a': a}
    _L2_gnn_all = _L2_gnn_setup()
    _L2_gnn_in = {k: v for k, v in _L2_gnn_all.items() if k in ('W', 'a')}
    del _L2_gnn_all

    def _L3_gnn_setup():
        import jax, jax.numpy as jnp
        import numpy as np
        NEG_BIG = -9000000000000000.0
        key = jax.random.key(seed)
        k1, k2, k3, k4 = jax.random.split(key, 4)
        B, N, F_in, F_out = (4, 2048, 128, 128)
        h = jax.random.normal(k1, (B, N, F_in), dtype=jnp.float32)
        adj = jax.random.randint(k2, (B, N, N), 0, 2, dtype=jnp.int32)
        bW = 1.414 * np.sqrt(6.0 / (F_in + F_out))
        W = jax.random.uniform(k3, (F_in, F_out), minval=-bW, maxval=bW, dtype=jnp.float32)
        ba = 1.414 * np.sqrt(6.0 / (2 * F_out + 1))
        a = jax.random.uniform(k4, (2 * F_out, 1), minval=-ba, maxval=ba, dtype=jnp.float32)
        return {'h': h, 'adj': adj, 'W': W, 'a': a}
    _L3_gnn_all = _L3_gnn_setup()
    _L3_gnn_in = {k: v for k, v in _L3_gnn_all.items() if k in ('W', 'a')}
    del _L3_gnn_all
    return {'x': x, 'adj': adj, 'nodemask': nodemask, 'L0_gnn_weight': _L0_gnn_in['weight'], 'L0_gnn_w_ih': _L0_gnn_in['w_ih'], 'L0_gnn_w_hh': _L0_gnn_in['w_hh'], 'L0_gnn_b_ih': _L0_gnn_in['b_ih'], 'L0_gnn_b_hh': _L0_gnn_in['b_hh'], 'L1_gnn_Wq': _L1_gnn_in['Wq'], 'L1_gnn_Wk': _L1_gnn_in['Wk'], 'L1_gnn_Wv': _L1_gnn_in['Wv'], 'L1_gnn_Wo': _L1_gnn_in['Wo'], 'L1_gnn_bo': _L1_gnn_in['bo'], 'L2_gnn_W': _L2_gnn_in['W'], 'L2_gnn_a': _L2_gnn_in['a'], 'L3_gnn_W': _L3_gnn_in['W'], 'L3_gnn_a': _L3_gnn_in['a']}

def reference(x, adj, nodemask, L0_gnn_weight, L0_gnn_w_ih, L0_gnn_w_hh, L0_gnn_b_ih, L0_gnn_b_hh, L1_gnn_Wq, L1_gnn_Wk, L1_gnn_Wv, L1_gnn_Wo, L1_gnn_bo, L2_gnn_W, L2_gnn_a, L3_gnn_W, L3_gnn_a):
    import jax
    import jax.numpy as jnp

    def _L0_gnn_ref(x, adj, weight, w_ih, w_hh, b_ih, b_hh):
        import jax, jax.numpy as jnp
        import numpy as np
        OUT = 128
        NUM_LAYERS = 3

        def _gru_cell(inp, h, w_ih, w_hh, b_ih, b_hh):
            gi = inp @ w_ih.T + b_ih
            gh = h @ w_hh.T + b_hh
            i_r, i_z, i_n = jnp.split(gi, 3, axis=-1)
            h_r, h_z, h_n = jnp.split(gh, 3, axis=-1)
            r = jax.nn.sigmoid(i_r + h_r)
            z = jax.nn.sigmoid(i_z + h_z)
            n = jnp.tanh(i_n + r * h_n)
            return (1.0 - z) * n + z * h
        A = (adj != 0).astype(x.dtype)
        h = x
        L = weight.shape[0]
        for i in range(L):
            m = jnp.einsum('bnd,de->bne', h, weight[i])
            aggr = jnp.einsum('bst,bsd->btd', A, m)
            h = _gru_cell(aggr, h, w_ih, w_hh, b_ih, b_hh)
        return h

    def _L1_gnn_ref(node_features, adjacency_matrix, Wq, Wk, Wv, Wo, bo):
        import jax, jax.numpy as jnp
        import numpy as np
        UNITS = 128
        NUM_HEADS = 8
        HEAD_DIM = UNITS // NUM_HEADS
        B, N = (8, 1024)
        b, n, _ = node_features.shape
        h, d = (NUM_HEADS, HEAD_DIM)
        q = (node_features @ Wq).reshape(b, n, h, d).transpose(0, 2, 1, 3)
        k = (node_features @ Wk).reshape(b, n, h, d).transpose(0, 2, 1, 3)
        v = (node_features @ Wv).reshape(b, n, h, d).transpose(0, 2, 1, 3)
        scores = jnp.einsum('bhqd,bhkd->bhqk', q, k) / jnp.sqrt(jnp.float32(d))
        mask = adjacency_matrix[:, None, :, :] > 0
        scores = jnp.where(mask, scores, jnp.float32(-1000000000.0))
        w = jax.nn.softmax(scores, axis=-1)
        ctx = jnp.einsum('bhqk,bhkd->bhqd', w, v)
        ctx = ctx.transpose(0, 2, 1, 3).reshape(b, n, h * d)
        return ctx @ Wo + bo

    def _L2_gnn_ref(h, adj, mask, W, a):
        import jax, jax.numpy as jnp
        import numpy as np
        ALPHA = 0.2
        NEG_BIG = -9000000000000000.0
        Fout = W.shape[1]
        Wh = jnp.einsum('bni,io->bno', h, W)
        a1 = a[:Fout, 0]
        a2 = a[Fout:, 0]
        f1 = Wh @ a1
        f2 = Wh @ a2
        e = jax.nn.leaky_relu(f1[:, :, None] + f2[:, None, :], negative_slope=ALPHA)
        scores = jnp.where(adj > 0, e, NEG_BIG)
        attention = jax.nn.softmax(scores, axis=2)
        h_prime = jnp.einsum('bij,bjo->bio', attention, Wh)
        h_prime = h_prime * mask[:, :, None]
        return jax.nn.elu(h_prime)

    def _L3_gnn_ref(h, adj, W, a):
        import jax, jax.numpy as jnp
        import numpy as np
        NEG_BIG = -9000000000000000.0
        F_out = W.shape[1]
        Wh = jnp.einsum('bnf,fo->bno', h, W)
        src = Wh @ a[:F_out, 0]
        dst = Wh @ a[F_out:, 0]
        e = jax.nn.leaky_relu(src[:, :, None] + dst[:, None, :], negative_slope=0.2)
        scores = jnp.where(adj > 0, e, jnp.float32(NEG_BIG))
        attention = jax.nn.softmax(scores, axis=2)
        h_prime = jnp.einsum('bij,bjo->bio', attention, Wh)
        return jax.nn.relu(h_prime)
    h = jnp.maximum(_layernorm(x, axis=-1), 0.0)
    x = x + _L0_gnn_ref(h, adj, L0_gnn_weight, L0_gnn_w_ih, L0_gnn_w_hh, L0_gnn_b_ih, L0_gnn_b_hh)
    h = jnp.maximum(_layernorm(x, axis=-1), 0.0)
    x = x + _L1_gnn_ref(h, adj, L1_gnn_Wq, L1_gnn_Wk, L1_gnn_Wv, L1_gnn_Wo, L1_gnn_bo)
    h = jnp.maximum(_layernorm(x, axis=-1), 0.0)
    x = x + _L2_gnn_ref(h, adj, nodemask, L2_gnn_W, L2_gnn_a)
    h = jnp.maximum(_layernorm(x, axis=-1), 0.0)
    x = x + _L3_gnn_ref(h, adj, L3_gnn_W, L3_gnn_a)
    return x

_drawn_inputs = setup_inputs


def setup_inputs(seed=0):
    import zlib

    import numpy as np

    out = dict(_drawn_inputs(seed))
    spreads = {'L1_gnn_bo': (0.0, 0.1)}
    factors = {}
    for name, (base, spread) in spreads.items():
        noise = np.random.default_rng([zlib.crc32(name.encode()), seed]).standard_normal(out[name].shape)
        drawn = base * np.exp(spread * noise) if base else spread * noise
        out[name] = jnp.asarray(drawn.astype(out[name].dtype))
    for name, factor in factors.items():
        out[name] = (out[name] * factor).astype(out[name].dtype)
    return out
```

```python
from contextlib import ExitStack

import concourse.bass as bass
from concourse import mybir

F32, BF16, I32 = mybir.dt.float32, mybir.dt.bfloat16, mybir.dt.int32
ACT = mybir.ActivationFunctionType
ALU = mybir.AluOpType

P = 128
G, N, D = 8, 1024, 128
T = N // P
HALF = N // 2
TH = T // 2
LAYERS = 3
HEADS, HD = 8, 16
PAIRS = HEADS // 2
SLOT = 32
SLOPE = 0.2
EPS = 1e-5
NO_EDGE = -float(2 ** 100)
LOWEST = -3.0e38
NEWTON = 4
STAGES = 4
PROBS = 16
OW = 132


def build(nc, x, adj, adj_t, nodemask, w0, wih_t, whh_t, bih, bhh, wq, wk, wv, wo, bo, kbias,
          gat_w, gat_a, gat_arep, ident, slot_sum, slot_first, out):
    with ExitStack() as ctx:
        def sb(name, shape, dt=F32):
            return ctx.enter_context(nc.sbuf_tensor(name, shape, dt))

        def sem(name):
            return ctx.enter_context(nc.semaphore(name))

        w0_s = sb("w0_s", [P, LAYERS, D])
        wih_s = sb("wih_s", [P, 3 * D])
        whh_s = sb("whh_s", [P, 3 * D])
        bih_s = sb("bih_s", [P, 3])
        bhh_s = sb("bhh_s", [P, 3])
        brz_s = sb("brz_s", [P, 3])
        wq_s = sb("wq_s", [P, PAIRS, P])
        wk_s = sb("wk_s", [P, PAIRS, P])
        wv_s = sb("wv_s", [P, D])
        wo_s = sb("wo_s", [P, PAIRS, 2, D])
        bo_s = sb("bo_s", [P, D])
        kbias_s = sb("kbias_s", [P, 1])
        gw_s = sb("gw_s", [P, 2, D])
        ga_s = sb("ga_s", [P, 2, 2])
        garep_s = sb("garep_s", [P, 2, 2, P])
        ident_s = sb("ident_s", [P, P])
        identb_s = sb("identb_s", [P, P], BF16)
        slotsum_s = sb("slotsum_s", [P, P])
        first_s = sb("first_s", [P, P])
        ones_s = sb("ones_s", [P, P])
        mask_s = sb("mask_s", [P, T])
        edge01 = sb("edge01", [P, T, N], BF16)
        noedge = sb("noedge", [P, T, N], BF16)
        noedge_t = sb("noedge_t", [P, T, N], BF16)
        stage = sb("stage", [P, STAGES, N], I32)
        xs = sb("xs", [P, T, D])
        xn = sb("xn", [P, T, D])
        hT = sb("hT", [P, N])
        stats = sb("stats", [P, T, 6])
        mv = sb("mv", [P, T, 2])
        nt1 = sb("nt1", [P, T]); nt2 = sb("nt2", [P, T]); nt3 = sb("nt3", [P, T])
        seed = sb("seed", [P, T], I32)
        m1 = sb("m1", [P, N], BF16); m2 = sb("m2", [P, N], BF16); m3 = sb("m3", [P, N], BF16)
        work = sb("work", [P, PROBS, HALF])
        qk = sb("qk", [P, 2 * PAIRS, N])
        vp = sb("vp", [P, T, HEADS, SLOT])
        mpad = sb("mpad", [P, 2, T, P])
        pvs = sb("pvs", [P, 2, HALF])
        rl = sb("rl", [P, HALF])
        ctxn = sb("ctxn", [P, PAIRS, HALF])
        junk = sb("junk", [P, 2, N], BF16)
        wh = sb("wh", [P, T, OW])
        fcol = sb("fcol", [P, T, 2])
        mf2 = sb("mf2", [P, T]); gx = sb("gx", [P, T]); gm = sb("gm", [P, T])
        rinv = sb("rinv", [P, T])
        psum = ctx.enter_context(nc.psum_tensor("banks", [P, 8, HALF], F32))

        def two_banks(k):
            return psum[:, k:k + 2, :].rearrange("p a b -> p (a b)")

        workn = work[:, :, :].rearrange("p (a b) n -> p a (b n)", b=2)
        res1, aggT, rT, zT, tT, nT = (workn[:, k, :] for k in range(6))
        qT = qk[:, 0:PAIRS, :]
        kT = qk[:, PAIRS:2 * PAIRS, :]
        whT, f1row, mrow, diag = (qk[:, k, :] for k in range(4))
        gup, gmin, gexp = (workn[:, k, :] for k in range(5, 8))

        weights_in = sem("weights_in")
        consts_ready, vp_zeroed = sem("consts_ready"), sem("vp_zeroed")
        pre_in, pre_done = sem("pre_in"), sem("pre_done")
        graph_done, cleared, resumed = sem("graph_done"), sem("cleared"), sem("resumed")
        names = ("x_in stored chain norm_ready turned hT_ready noedge_ready edge_ready "
                 "msg_ready m1_ready res_ready m2_ready m3_ready agg_ready aggT_ready hn_ready r_ready "
                 "n_ready z_ready rT_ready zT_ready t_ready nT_ready h_ready back_ready "
                 "quad_ready quad_free v_psum v_ready score_ready prob_ready pv_done pair_saved "
                 "whT_psum wh_psum whT_ready wh_ready f2_ready fcol_ready f1_psum f1_ready fcol_saved "
                 "diag_ready mrow_psum mrow_ready gscore_ready gsum_ready lrelu_ready shifted_ready gprob_ready "
                 "gpv_step gout_ready elu_in elu_out result_ready").split()
        S = {n: sem(n) for n in names}
        stage_in = [sem(f"stage_in{k}") for k in range(STAGES)]
        stage_used = [sem(f"stage_used{k}") for k in range(STAGES)]
        per_graph = list(S.values()) + stage_in + stage_used

        def end_graph(eng, g):
            eng.drain().then_inc(graph_done, 1)
            eng.wait_ge(cleared, g + 1)
            eng.sem_inc(resumed, 1)

        quad_order = [("proj", 0), ("proj", 1)] + [("s", 0, t) for t in range(T)] + [("max", 0)]
        stage_uses = []
        for hp in range(PAIRS):
            uses = []
            if hp + 2 < PAIRS:
                uses.append(("proj", hp + 2))
            if hp + 1 < PAIRS:
                uses += [("s", hp + 1, t) for t in range(T)] + [("max", hp + 1)]
            if hp >= 1:
                uses.append(("sum", hp - 1))
            stage_uses.append(uses)
            quad_order += uses
        quad_order += [("sum", PAIRS - 1), ("wo",)]
        quad_at = {u: n for n, u in enumerate(quad_order)}

        block = ctx.enter_context(nc.Block())

        loads = [(w0_s[:], w0.rearrange("l d e -> d l e")), (wih_s[:], wih_t), (whh_s[:], whh_t),
                 (bih_s[:], bih), (bhh_s[:], bhh), (wq_s[:], wq), (wk_s[:], wk), (wv_s[:], wv), (wo_s[:], wo),
                 (bo_s[:], bo), (kbias_s[:], kbias), (gw_s[:], gat_w), (ga_s[:], gat_a),
                 (garep_s[:], gat_arep), (ident_s[:], ident), (slotsum_s[:], slot_sum), (first_s[:], slot_first)]

        @block.sync
        def _(sp):
            for dst, src in loads:
                sp.dma_start(dst, src).then_inc(weights_in, 16)
            for t in range(T):
                if t >= STAGES and t % STAGES == 0:
                    sp.wait_ge(pre_done, t)
                sp.dma_start(stage[:, t % STAGES, :], adj[0, t * P:(t + 1) * P, :]).then_inc(pre_in, 16)
            sp.wait_ge(pre_done, T)
            with sp.Fori(0, G) as g:
                sp.dma_start(xs[:, :, :], x[bass.ds(g, 1)].rearrange("o (t p) d -> p (o t) d", p=P)).then_inc(S["x_in"], 16)
                sp.dma_start(mask_s[:, :], nodemask[bass.ds(g, 1)].rearrange("o p t -> p (o t)")).then_inc(S["x_in"], 16)
                nxt = (g + 1) % G
                for n in range(3 * T):
                    k, t = n % STAGES, n % T
                    if n >= STAGES:
                        sp.wait_ge(stage_used[k], n // STAGES)
                    src = (adj[bass.ds(g, 1)], adj_t[bass.ds(g, 1)], adj[bass.ds(nxt, 1)])[n // T]
                    sp.dma_start(stage[:, k, :], src[:, t * P:(t + 1) * P, :].rearrange("o p n -> (o p) n")
                                 ).then_inc(stage_in[k], 16)
                sp.wait_ge(S["result_ready"], 1)
                sp.dma_start(out[bass.ds(g, 1)].rearrange("o (t p) d -> p (o t) d", p=P), xs[:, :, :]
                             ).then_inc(S["stored"], 16)
                sp.wait_ge(S["stored"], 16)
                end_graph(sp, g)

        @block.gpsimd
        def _(pool):
            pool.memset(ones_s[:], 1.0).then_inc(consts_ready, 1)
            pool.memset(vp[:, :, :, :], 0.0).then_inc(vp_zeroed, 1)
            pool.memset(mpad[:, :, :, :], 0.0).then_inc(consts_ready, 1)
            pool.memset(wh[:, :, D:OW], 1.0).then_inc(consts_ready, 1)
            pool.wait_ge(vp_zeroed, 1)
            pool.memset(vp[:, :, :, HD:HD + 1], 1.0).then_inc(consts_ready, 1)
            with pool.Fori(0, G) as g:
                for n in range(2 * T):
                    k, t = n % STAGES, n % T
                    pool.wait_ge(stage_in[k], 16 * (n // STAGES + 1))
                    dst = (noedge, noedge_t)[n // T]
                    pool.tensor_scalar(dst[:, t, :], stage[:, k, :], 0.0, NO_EDGE, ALU.is_le, ALU.mult
                                       ).then_inc(stage_used[k], 1)
                pool.sem_inc(resumed, 1)
                pool.wait_ge(graph_done, 4 * (g + 1))
                pool.sem_inc(resumed, 1)
                for s in per_graph:
                    pool.sem_clear(s)
                pool.sem_inc(cleared, 1)
                pool.wait_ge(cleared, g + 1)
                pool.sem_inc(resumed, 1)

        def stage_tiles_done(eng, upto):
            for k in range(STAGES):
                eng.wait_ge(stage_used[k], (upto - k + STAGES - 1) // STAGES)

        @block.vector
        def _(dve):
            v = nc.vector
            dve.wait_ge(weights_in, 16 * len(loads))
            v.tensor_copy(identb_s[:], ident_s[:]).then_inc(consts_ready, 1)
            v.tensor_tensor(brz_s[:], bih_s[:], bhh_s[:], ALU.add).then_inc(consts_ready, 1)
            for t in range(T):
                if t % STAGES == 0:
                    dve.wait_ge(pre_in, 16 * (t + STAGES))
                v.tensor_scalar(edge01[:, t, :], stage[:, t % STAGES, :], 0.0, None, ALU.not_equal).then_inc(pre_done, 1)

            with dve.Fori(0, G) as g:
                links = [0]

                def link(ins):
                    links[0] += 1
                    ins.then_inc(S["chain"], 1)
                    dve.wait_ge(S["chain"], links[0])

                def normalise(k):
                    for t in range(T):
                        last = v.bn_stats(stats[:, t, :], xs[:, t, :])
                    link(last)
                    for t in range(T):
                        last = v.bn_aggr(mv[:, t, :], stats[:, t, :])
                    link(last)
                    link(v.tensor_scalar(nt1[:], mv[:, :, 1], EPS, None, ALU.add))
                    link(v.tensor_scalar(seed[:], nt1[:].bitcast(I32), 1, None, ALU.arith_shift_right))
                    link(v.tensor_scalar(seed[:], seed[:], -1.0, float(0x5F3759DF), ALU.mult, ALU.add))
                    y, y_next = seed[:].bitcast(F32), nt3[:]
                    for _ in range(NEWTON):
                        link(v.tensor_tensor(nt2[:], y, y, ALU.mult))
                        link(v.scalar_tensor_tensor(out=nt2[:], in0=nt2[:], scalar=-0.5, in1=nt1[:],
                                                    op0=ALU.mult, op1=ALU.mult))
                        link(v.scalar_tensor_tensor(out=y_next, in0=nt2[:], scalar=1.5, in1=y,
                                                    op0=ALU.add, op1=ALU.mult))
                        y, y_next = y_next, y
                    for t in range(T):
                        v.tensor_scalar(xn[:, t, :], xs[:, t, :], mv[:, t, 0:1], y[:, t:t + 1],
                                        ALU.subtract, ALU.mult).then_inc(S["norm_ready"], 1)

                dve.wait_ge(S["x_in"], 32)
                normalise(0)
                for l in range(LAYERS):
                    for h in range(2):
                        c = slice(h * HALF, (h + 1) * HALF)
                        dve.wait_ge(S["m1_ready"], 2 * l + h + 1)
                        v.tensor_tensor(res1[:, c], psum[:, h, :], m1[:, c], ALU.subtract).then_inc(S["res_ready"], 1)
                    for h in range(2):
                        c = slice(h * HALF, (h + 1) * HALF)
                        dve.wait_ge(S["m2_ready"], 2 * l + h + 1)
                        v.tensor_tensor(m3[:, c], res1[:, c], m2[:, c], ALU.subtract).then_inc(S["m3_ready"], 1)
                    for h in range(2):
                        c = slice(h * HALF, (h + 1) * HALF)
                        dve.wait_ge(S["rT_ready"], 2 * l + h + 1)
                        dve.wait_ge(S["hn_ready"], 2 * l + h + 1)
                        link(v.scalar_tensor_tensor(out=tT[:, c], in0=psum[:, h, :], scalar=bhh_s[:, 2:3], in1=rT[:, c],
                                                    op0=ALU.add, op1=ALU.mult))
                        dve.wait_ge(S["n_ready"], 2 * l + h + 1)
                        v.tensor_tensor(tT[:, c], psum[:, 2 + h, :], tT[:, c], ALU.add).then_inc(S["t_ready"], 1)
                    for h in range(2):
                        c = slice(h * HALF, (h + 1) * HALF)
                        dve.wait_ge(S["nT_ready"], 2 * l + h + 1)
                        link(v.tensor_tensor(tT[:, c], hT[:, c], nT[:, c], ALU.subtract))
                        dve.wait_ge(S["zT_ready"], 2 * l + h + 1)
                        link(v.tensor_tensor(tT[:, c], tT[:, c], zT[:, c], ALU.mult))
                        v.tensor_tensor(hT[:, c], tT[:, c], nT[:, c], ALU.add).then_inc(S["h_ready"], 1)
                for h in range(2):
                    dve.wait_ge(S["back_ready"], h + 1)
                    o = xs[:, h * TH:(h + 1) * TH, :].rearrange("p t d -> p (t d)")
                    last = v.tensor_tensor(o, psum[:, h, :], o, ALU.add)
                link(last)

                normalise(1)
                def empty(use):
                    n, kind = quad_at[use], use[0]
                    if kind == "proj":
                        hp = use[1]
                        dve.wait_ge(S["quad_ready"], 2 * n + 1)
                        v.tensor_scalar(qT[:, hp, :], two_banks(0), HD ** -0.5, None, ALU.mult).then_inc(S["quad_free"], 1)
                        dve.wait_ge(S["quad_ready"], 2 * n + 2)
                        v.tensor_scalar(kT[:, hp, :], two_banks(2), kbias_s[:, 0:1], None, ALU.add).then_inc(S["quad_free"], 1)
                    elif kind == "s":
                        _, hp, t = use
                        for a in range(2):
                            dve.wait_ge(S["quad_ready"], 2 * n + a + 1)
                            dve.wait_ge(S["quad_free"], 2 * n + a - 1)
                            col = SLOT * (2 * a + t // TH) + HD
                            v.tensor_tensor_reduce(junk[:, a, :], two_banks(2 * a), noedge[:, t, :], 1.0, LOWEST,
                                                   ALU.add, ALU.max, mpad[:, hp % 2, t, col:col + 1]
                                                   ).then_inc(S["quad_free"], 1)
                    elif kind == "max":
                        hp = use[1]
                        for h in range(2):
                            c = slice(h * HALF, (h + 1) * HALF)
                            dve.wait_ge(S["quad_ready"], 2 * n + h + 1)
                            v.tensor_tensor(qT[:, hp, c], psum[:, h, :], qT[:, hp, c], ALU.add).then_inc(S["quad_free"], 1)
                    elif kind == "sum":
                        hp = use[1]
                        dve.wait_ge(S["quad_ready"], 2 * n + 2)
                        v.reciprocal(rl[:], psum[:, 0, :]).then_inc(S["quad_free"], 1)
                        dve.wait_ge(S["quad_free"], 2 * n + 1)
                        v.tensor_tensor(ctxn[:, hp, :], pvs[:, hp % 2, :], rl[:], ALU.mult).then_inc(S["quad_free"], 1)

                for use in quad_order[:-2]:
                    if use == ("s", 1, 0):
                        pass
                    if use == ("s", 0, 0):
                        stage_tiles_done(dve, T)
                    empty(use)
                    if use[0] == "s" and use[1] == 2:
                        n = 2 * T + use[2]
                        dve.wait_ge(stage_in[n % STAGES], 16 * (n // STAGES + 1))
                        v.tensor_scalar(edge01[:, use[2], :], stage[:, n % STAGES, :], 0.0, None, ALU.not_equal
                                        ).then_inc(stage_used[n % STAGES], 1)
                xs_flat = xs[:, :, :].rearrange("p t d -> p (t d)")
                link(v.tensor_tensor(xs[:, :, :], xs[:, :, :], bo_s[:, None, :].to_broadcast([P, T, D]), ALU.add))
                empty(("sum", PAIRS - 1))
                n = quad_at[("wo",)]
                for h in range(2):
                    dve.wait_ge(S["quad_ready"], 2 * n + h + 1)
                    o = xs[:, h * TH:(h + 1) * TH, :].rearrange("p t d -> p (t d)")
                    last = v.tensor_tensor(o, psum[:, h, :], o, ALU.add)
                link(last)

                for k in range(2):
                    normalise(2 + k)
                    for h in range(2):
                        dve.wait_ge(S["wh_psum"], 2 * k + h + 1)
                        v.tensor_copy(wh[:, h * TH:(h + 1) * TH, 0:D],
                                      psum[:, 2 + h, :].rearrange("p (t d) -> p t d", d=D)).then_inc(S["wh_ready"], 1)
                    dve.wait_ge(S["fcol_ready"], k + 1)
                    v.tensor_copy(fcol[:, :, :].rearrange("p t c -> p (t c)"), psum[:, 0, 0:2 * T]).then_inc(S["fcol_saved"], 1)
                    dve.wait_ge(S["f2_ready"], k + 1)
                    for t in range(T):
                        if t >= 2:
                            dve.wait_ge(S["chain"], links[0] - 1)
                        v.tensor_tensor_reduce(junk[:, t % 2, :], two_banks(5), noedge[:, t, :], 1.0, LOWEST,
                                               ALU.add, ALU.max, mf2[:, t:t + 1]).then_inc(S["chain"], 1)
                        links[0] += 1
                    dve.wait_ge(S["chain"], links[0])
                    dve.wait_ge(S["fcol_saved"], k + 1)
                    link(v.tensor_tensor(gx[:], mf2[:], fcol[:, :, 0], ALU.add))
                    link(v.scalar_tensor_tensor(out=gm[:], in0=gx[:], scalar=SLOPE, in1=gx[:], op0=ALU.mult, op1=ALU.max))
                    v.tensor_tensor(diag.rearrange("p (t n) -> p t n", t=T), ident_s[:, None, :].to_broadcast([P, T, P]),
                                    gm[:, :, None].to_broadcast([P, T, P]), ALU.mult).then_inc(S["diag_ready"], 1)
                    dve.wait_ge(S["mrow_ready"], 2 * (k + 1))

                    def lrelu(t):
                        dve.wait_ge(S["gsum_ready"], k * T + t + 1)
                        y = workn[:, t % 2, :]
                        v.scalar_tensor_tensor(out=y, in0=y, scalar=SLOPE, in1=y, op0=ALU.mult, op1=ALU.max
                                               ).then_inc(S["lrelu_ready"], 1)

                    lrelu(0)
                    for t in range(T):
                        if t + 1 < T:
                            lrelu(t + 1)
                        dve.wait_ge(S["lrelu_ready"], k * T + t + 1)
                        y = workn[:, t % 2, :]
                        v.tensor_tensor(y, y, mrow, ALU.subtract).then_inc(S["shifted_ready"], 1)
                    dve.wait_ge(S["gpv_step"], T * (k + 1))
                    for b in range(3):
                        nb = min(3, T - 3 * b)
                        o = psum[:, 5 + b, 0:nb * OW].rearrange("p (t c) -> p t c", c=OW)
                        last = v.reciprocal(rinv[:, 3 * b:3 * b + nb], o[:, :, D])
                    link(last)
                    if k == 0:
                        link(v.tensor_tensor(rinv[:], rinv[:], mask_s[:], ALU.mult))
                    up = gup.rearrange("p (t d) -> p t d", t=T)
                    for b in range(3):
                        nb = min(3, T - 3 * b)
                        o = psum[:, 5 + b, 0:nb * OW].rearrange("p (t c) -> p t c", c=OW)
                        last = v.tensor_tensor(up[:, 3 * b:3 * b + nb, :], o[:, :, 0:D],
                                               rinv[:, 3 * b:3 * b + nb, None].to_broadcast([P, nb, D]), ALU.mult)
                    last.then_inc(S["gout_ready"], 1)
                    dve.wait_ge(S["gout_ready"], k + 1)
                    if k == 0:
                        v.tensor_scalar(gmin, gup, 0.0, None, ALU.min).then_inc(S["elu_in"], 1)
                        link(v.scalar_tensor_tensor(out=xs_flat, in0=gup, scalar=0.0, in1=xs_flat, op0=ALU.max, op1=ALU.add))
                        dve.wait_ge(S["elu_out"], 1)
                        link(v.scalar_tensor_tensor(out=xs_flat, in0=gexp, scalar=-1.0, in1=xs_flat, op0=ALU.add, op1=ALU.add))
                    else:
                        v.scalar_tensor_tensor(out=xs_flat, in0=gup, scalar=0.0, in1=xs_flat, op0=ALU.max, op1=ALU.add
                                               ).then_inc(S["result_ready"], 1)
                end_graph(dve, g)

        @block.scalar
        def _(act):
            a = nc.scalar

            def turn_in(k):
                for h in range(2):
                    act.wait_ge(S["turned"], 2 * k + h + 1)
                    a.activation(hT[:, h * HALF:(h + 1) * HALF], psum[:, h, :], ACT.Relu).then_inc(S["hT_ready"], 1)

            act.wait_ge(consts_ready, 6)
            with act.Fori(0, G) as g:
                turn_in(0)
                for l in range(LAYERS):
                    for h in range(2):
                        c = slice(h * HALF, (h + 1) * HALF)
                        act.wait_ge(S["msg_ready"], 2 * l + h + 1)
                        a.copy(m1[:, c], psum[:, h, :]).then_inc(S["m1_ready"], 1)
                    for h in range(2):
                        c = slice(h * HALF, (h + 1) * HALF)
                        act.wait_ge(S["res_ready"], 2 * l + h + 1)
                        a.copy(m2[:, c], res1[:, c]).then_inc(S["m2_ready"], 1)
                    for h in range(2):
                        c = slice(h * HALF, (h + 1) * HALF)
                        act.wait_ge(S["agg_ready"], 2 * l + h + 1)
                        a.copy(aggT[:, c], psum[:, 2 + h, :]).then_inc(S["aggT_ready"], 1)
                    for h in range(2):
                        c = slice(h * HALF, (h + 1) * HALF)
                        act.wait_ge(S["r_ready"], 2 * l + h + 1)
                        a.activation(rT[:, c], psum[:, 4 + h, :], ACT.Sigmoid, bias=brz_s[:, 0:1]).then_inc(S["rT_ready"], 1)
                        act.wait_ge(S["z_ready"], 2 * l + h + 1)
                        a.activation(zT[:, c], psum[:, 6 + h, :], ACT.Sigmoid, bias=brz_s[:, 1:2]).then_inc(S["zT_ready"], 1)
                    for h in range(2):
                        c = slice(h * HALF, (h + 1) * HALF)
                        act.wait_ge(S["t_ready"], 2 * l + h + 1)
                        a.activation(nT[:, c], tT[:, c], ACT.Tanh, bias=bih_s[:, 2:3]).then_inc(S["nT_ready"], 1)

                turn_in(1)
                act.wait_ge(S["v_psum"], 2)
                a.copy(vp[:, :, :, 0:HD], two_banks(4).rearrange("p (t h d) -> p t h d", t=T, h=HEADS)).then_inc(S["v_ready"], 1)
                for hp in range(PAIRS):
                    for u in range(4 * T):
                        n = 4 * T * hp + u
                        act.wait_ge(S["score_ready"], n + 1)
                        if n >= PROBS:
                            act.wait_ge(S["pv_done"], (n - PROBS) // 4 + 1)
                        a.activation(work[:, n % PROBS, :], psum[:, 4 + n % 3, :], ACT.Exp).then_inc(S["prob_ready"], 1)
                        if hp >= 1 and u == 3:
                            act.wait_ge(S["pv_done"], T * hp)
                            if hp >= 3:
                                act.wait_ge(S["quad_free"], 2 * quad_at[("sum", hp - 3)] + 2)
                            a.copy(pvs[:, (hp - 1) % 2, :], psum[:, 7, :]).then_inc(S["pair_saved"], 1)
                act.wait_ge(S["pv_done"], T * PAIRS)
                act.wait_ge(S["quad_free"], 2 * quad_at[("sum", PAIRS - 3)] + 2)
                a.copy(pvs[:, (PAIRS - 1) % 2, :], psum[:, 7, :]).then_inc(S["pair_saved"], 1)

                for k in range(2):
                    turn_in(2 + k)
                    for h in range(2):
                        act.wait_ge(S["whT_psum"], 2 * k + h + 1)
                        a.copy(whT[:, h * HALF:(h + 1) * HALF], psum[:, h, :]).then_inc(S["whT_ready"], 1)
                    for h in range(2):
                        act.wait_ge(S["f1_psum"], 2 * k + h + 1)
                        a.copy(f1row[:, h * HALF:(h + 1) * HALF], psum[:, (4, 7)[h], :]).then_inc(S["f1_ready"], 1)

                    def add_f2(t):
                        act.wait_ge(S["gscore_ready"], k * T + t + 1)
                        act.wait_ge(S["fcol_saved"], k + 1)
                        if t >= 2:
                            act.wait_ge(S["gprob_ready"], k * T + t - 1)
                        a.activation(workn[:, t % 2, :], two_banks(1 + 2 * (t % 2)), ACT.Identity,
                                     bias=fcol[:, t, 1:2]).then_inc(S["gsum_ready"], 1)

                    add_f2(0)
                    for h in range(2):
                        act.wait_ge(S["mrow_psum"], 2 * k + h + 1)
                        a.copy(mrow[:, h * HALF:(h + 1) * HALF], psum[:, (0, 7)[h], :]).then_inc(S["mrow_ready"], 1)
                    add_f2(1)
                    for t in range(T):
                        act.wait_ge(S["shifted_ready"], k * T + t + 1)
                        if t >= 2:
                            act.wait_ge(S["gpv_step"], k * T + t - 1)
                        a.activation(workn[:, 2 + t % 2, :], workn[:, t % 2, :], ACT.Exp).then_inc(S["gprob_ready"], 1)
                        if t + 2 < T:
                            add_f2(t + 2)
                    if k == 0:
                        act.wait_ge(S["elu_in"], 1)
                        a.activation(gexp, gmin, ACT.Exp).then_inc(S["elu_out"], 1)
                end_graph(act, g)

        @block.tensor
        def _(pe):
            mm = nc.tensor.matmul

            def turn_out(k):
                for h in range(2):
                    pe.wait_ge(S["norm_ready"], k * T + (h + 1) * TH)
                    for t in range(TH):
                        last = nc.tensor.transpose(psum[:, h, t * P:(t + 1) * P], xn[:, h * TH + t, :], ident_s[:])
                    last.then_inc(S["turned"], 1)

            pe.wait_ge(consts_ready, 6)
            with pe.Fori(0, G) as g:
                turn_out(0)
                for l in range(LAYERS):
                    for h in range(2):
                        if l == 0:
                            pe.wait_ge(S["hT_ready"], h + 1)
                            if h == 0:
                                pe.wait_ge(S["hT_ready"], 2)
                        else:
                            pe.wait_ge(S["h_ready"], 2 * (l - 1) + h + 1)
                        for t in range(TH):
                            last = mm(psum[:, h, t * P:(t + 1) * P], hT[:, (h * TH + t) * P:(h * TH + t + 1) * P],
                                      w0_s[:, l, :], start=True, stop=True)
                        last.then_inc(S["msg_ready"], 1)
                    for gate in range(2):
                        for h in range(2):
                            mm(psum[:, 4 + 2 * gate + h, :], whh_s[:, gate * D:(gate + 1) * D],
                               hT[:, h * HALF:(h + 1) * HALF], start=True, stop=False)
                    for part, (m, ready) in enumerate(((m1, "m1_ready"), (m2, "m2_ready"), (m3, "m3_ready"))):
                        for s in range(T):
                            if s % TH == 0:
                                pe.wait_ge(S[ready], 2 * l + s // TH + 1)
                            for h in range(2):
                                last = mm(psum[:, 2 + h, :], m[:, s * P:(s + 1) * P], edge01[:, s, h * HALF:(h + 1) * HALF],
                                          start=(part == 0 and s == 0), stop=(part == 2 and s == T - 1))
                                if part == 2 and s == T - 1:
                                    last.then_inc(S["agg_ready"], 1)
                    for h in range(2):
                        pe.wait_ge(S["res_ready"], 2 * l + h + 1)
                        mm(psum[:, h, :], whh_s[:, 2 * D:3 * D], hT[:, h * HALF:(h + 1) * HALF],
                           start=True, stop=True).then_inc(S["hn_ready"], 1)
                    for h in range(2):
                        c = slice(h * HALF, (h + 1) * HALF)
                        pe.wait_ge(S["aggT_ready"], 2 * l + h + 1)
                        mm(psum[:, 4 + h, :], wih_s[:, 0:D], aggT[:, c], start=False, stop=True).then_inc(S["r_ready"], 1)
                        mm(psum[:, 2 + h, :], wih_s[:, 2 * D:3 * D], aggT[:, c], start=True, stop=True).then_inc(S["n_ready"], 1)
                        mm(psum[:, 6 + h, :], wih_s[:, D:2 * D], aggT[:, c], start=False, stop=True).then_inc(S["z_ready"], 1)
                for h in range(2):
                    pe.wait_ge(S["h_ready"], 2 * (LAYERS - 1) + h + 1)
                    for t in range(TH):
                        last = nc.tensor.transpose(psum[:, h, t * P:(t + 1) * P],
                                                   hT[:, (h * TH + t) * P:(h * TH + t + 1) * P], ident_s[:])
                    last.then_inc(S["back_ready"], 1)

                turn_out(1)
                pe.wait_ge(S["hT_ready"], 4)

                def fill(use):
                    n, kind = quad_at[use], use[0]
                    if n:
                        pe.wait_ge(S["quad_free"], 2 * n)
                    if kind == "proj":
                        for b, w in enumerate((wq_s, wk_s)):
                            for h in range(2):
                                last = mm(psum[:, 2 * b + h, :], w[:, use[1], :], hT[:, h * HALF:(h + 1) * HALF],
                                          start=True, stop=True)
                            last.then_inc(S["quad_ready"], 1)
                    elif kind == "s":
                        _, hp, t = use
                        for j in range(4):
                            r = slice(SLOT * j, SLOT * (j + 1))
                            last = mm(psum[:, j, :], qT[r, hp, t * P:(t + 1) * P], kT[r, hp, (j % 2) * HALF:(j % 2 + 1) * HALF],
                                      start=True, stop=True)
                            if j % 2:
                                last.then_inc(S["quad_ready"], 1)
                    elif kind == "max":
                        for h in range(2):
                            for t in range(TH):
                                last = nc.tensor.transpose(psum[:, h, t * P:(t + 1) * P],
                                                           mpad[:, use[1] % 2, h * TH + t, :], ident_s[:])
                            last.then_inc(S["quad_ready"], 1)
                    elif kind == "sum":
                        hp = use[1]
                        pe.wait_ge(S["pair_saved"], hp + 1)
                        for h in range(2):
                            c = slice(h * HALF // 2, (h + 1) * HALF // 2)
                            mm(psum[:, 0, c], slotsum_s[:], pvs[:, hp % 2, c], start=True, stop=True).then_inc(S["quad_ready"], 1)
                    elif kind == "wo":
                        for t in range(T):
                            c = slice(t % TH * P, (t % TH + 1) * P)
                            for hp in range(PAIRS):
                                last = mm(psum[:, t // TH, c], ctxn[:, hp, c], wo_s[:, hp, t // TH, :],
                                          start=(hp == 0), stop=(hp == PAIRS - 1))
                            if t % TH == TH - 1:
                                last.then_inc(S["quad_ready"], 1)

                def values():
                    for h in range(2):
                        for t in range(TH):
                            last = mm(psum[:, 4 + h, t * P:(t + 1) * P], hT[:, (h * TH + t) * P:(h * TH + t + 1) * P],
                                      wv_s[:], start=True, stop=True)
                        last.then_inc(S["v_psum"], 1)

                def scores(hp, us):
                    for u in us:
                        n, kt, j = 4 * T * hp + u, u // 4, u % 4
                        if n >= 3:
                            pe.wait_ge(S["prob_ready"], n - 2)
                        mm(psum[:, 4 + n % 3, :], identb_s[:], noedge_t[:, kt, (j % 2) * HALF:(j % 2 + 1) * HALF],
                           start=True, stop=False, skip_group_check=True)
                    for u in us:
                        n, kt, j = 4 * T * hp + u, u // 4, u % 4
                        r = slice(SLOT * j, SLOT * (j + 1))
                        mm(psum[:, 4 + n % 3, :], kT[r, hp, kt * P:(kt + 1) * P], qT[r, hp, (j % 2) * HALF:(j % 2 + 1) * HALF],
                           start=False, stop=True, skip_group_check=True).then_inc(S["score_ready"], 1)

                def context(hp, kt):
                    n = T * hp + kt
                    pe.wait_ge(S["prob_ready"], 4 * n + 4)
                    if kt == 0 and hp >= 1:
                        pe.wait_ge(S["pair_saved"], hp)
                    for j in range(4):
                        last = mm(psum[SLOT * j:SLOT * (j + 1), 7, :], vp[:, kt, 2 * hp + j // 2, :],
                                  work[:, (4 * n + j) % PROBS, :], start=(kt == 0), stop=(kt == T - 1))
                    last.then_inc(S["pv_done"], 1)

                fill(("proj", 0))
                values()
                fill(("proj", 1))
                for t in range(T):
                    fill(("s", 0, t))
                fill(("max", 0))
                pe.wait_ge(S["v_ready"], 1)
                stage_tiles_done(pe, 2 * T)
                units = 4 * T
                for hp in range(PAIRS):
                    uses = list(stage_uses[hp])
                    pe.wait_ge(S["quad_free"], 2 * quad_at[("max", hp)] + 2)
                    done_kt = 0
                    for k, u in enumerate(range(0, units, 3)):
                        scores(hp, range(u, min(u + 3, units)))
                        if uses and (uses[0][0] != "sum" or k >= 3):
                            fill(uses.pop(0))
                        while 4 * done_kt + 3 < u:
                            context(hp, done_kt)
                            done_kt += 1
                    while done_kt < T:
                        context(hp, done_kt)
                        done_kt += 1
                    for use in uses:
                        fill(use)
                fill(("sum", PAIRS - 1))
                fill(("wo",))

                for k in range(2):
                    turn_out(2 + k)
                    pe.wait_ge(S["hT_ready"], 2 * (3 + k))
                    for h in range(2):
                        mm(psum[:, h, :], gw_s[:, k, :], hT[:, h * HALF:(h + 1) * HALF],
                           start=True, stop=True).then_inc(S["whT_psum"], 1)
                    for h in range(2):
                        for t in range(TH):
                            last = mm(psum[:, 2 + h, t * P:(t + 1) * P], hT[:, (h * TH + t) * P:(h * TH + t + 1) * P],
                                      gw_s[:, k, :], start=True, stop=True)
                        last.then_inc(S["wh_psum"], 1)
                    pe.wait_ge(S["whT_ready"], 2 * (k + 1))
                    for h in range(2):
                        last = mm(psum[:, 5 + h, :], garep_s[:, k, 1, :], whT[:, h * HALF:(h + 1) * HALF], start=True, stop=True)
                    last.then_inc(S["f2_ready"], 1)
                    for t in range(T):
                        last = mm(psum[:, 0, 2 * t:2 * t + 2], whT[:, t * P:(t + 1) * P], ga_s[:, k, :], start=True, stop=True)
                    last.then_inc(S["fcol_ready"], 1)
                    for h in range(2):
                        mm(psum[:, (4, 7)[h], :], garep_s[:, k, 0, :], whT[:, h * HALF:(h + 1) * HALF],
                           start=True, stop=True).then_inc(S["f1_psum"], 1)
                    pe.wait_ge(S["wh_ready"], 2 * (k + 1))
                    pe.wait_ge(S["f1_ready"], 2 * (k + 1))

                    def gat_scores(t):
                        if t >= 2:
                            pe.wait_ge(S["gsum_ready"], k * T + t - 1)
                        b = 1 + 2 * (t % 2)
                        for h in range(2):
                            mm(psum[:, b + h, :], identb_s[:], noedge_t[:, t, h * HALF:(h + 1) * HALF],
                               start=True, stop=False, skip_group_check=True)
                        for h in range(2):
                            r = slice(SLOT * (2 * (t % 2) + h), SLOT * (2 * (t % 2) + h + 1))
                            last = mm(psum[:, b + h, :], first_s[r, :], f1row[r, h * HALF:(h + 1) * HALF],
                                      start=False, stop=True, skip_group_check=True)
                        last.then_inc(S["gscore_ready"], 1)

                    gat_scores(0)
                    gat_scores(1)
                    pe.wait_ge(S["diag_ready"], k + 1)
                    pe.wait_ge(S["fcol_saved"], k + 1)
                    for h in range(2):
                        mm(psum[:, (0, 7)[h], :], ones_s[:], diag[:, h * HALF:(h + 1) * HALF],
                           start=True, stop=True).then_inc(S["mrow_psum"], 1)
                    pe.wait_ge(S["mrow_ready"], 2 * (k + 1))
                    for t in range(T):
                        pe.wait_ge(S["gprob_ready"], k * T + t + 1)
                        for i in range(T):
                            last = mm(psum[:, 5 + i // 3, (i % 3) * OW:(i % 3) * OW + D + 1],
                                      workn[:, 2 + t % 2, i * P:(i + 1) * P], wh[:, t, 0:D + 1],
                                      start=(t == 0 and i % 3 == 0), stop=(t == T - 1), skip_group_check=True)
                        last.then_inc(S["gpv_step"], 1)
                        if t + 2 < T:
                            gat_scores(t + 2)
                end_graph(pe, g)


def kernel(x, adj, nodemask, L0_gnn_weight, L0_gnn_w_ih, L0_gnn_w_hh, L0_gnn_b_ih, L0_gnn_b_hh,
           L1_gnn_Wq, L1_gnn_Wk, L1_gnn_Wv, L1_gnn_Wo, L1_gnn_bo, L2_gnn_W, L2_gnn_a, L3_gnn_W, L3_gnn_a):
    import numpy as np
    import concourse.bacc as bacc
    from concourse.bass_utils import run_bass_kernel_spmd as run

    def pair_columns(w):
        o = np.zeros((D, PAIRS, 4, SLOT), w.dtype)
        o[:, :, :, :HD] = np.repeat(w.reshape(D, PAIRS, 2, HD), 2, axis=2)
        return o.reshape(D, PAIRS, P)

    def pair_rows(w):
        o = np.zeros((PAIRS, 2, 2, 2, SLOT, D), w.dtype)
        rows = w.reshape(PAIRS, 2, HD, D)
        for b in range(2):
            o[:, b, :, b, :HD] = rows
        return o.reshape(PAIRS, 2, P, D).transpose(2, 0, 1, 3)

    f32 = np.float32
    row = np.arange(P)
    kbias = np.where(row % SLOT == HD, -1, 0).astype(f32).reshape(P, 1)
    slot_sum = ((row[:, None] % SLOT == HD) & (row[:, None] // SLOT == row[None, :] // SLOT)).astype(f32)
    slot_first = np.repeat((row % SLOT == 0).astype(f32)[:, None], P, axis=1)
    x, adj, nodemask = np.asarray(x), np.asarray(adj), np.asarray(nodemask)
    gat_a = [np.asarray(a).reshape(2, D) for a in (L2_gnn_a, L3_gnn_a)]
    arrays = {
        "x": x, "adj": adj, "adj_t": adj.transpose(0, 2, 1),
        "nodemask": nodemask.reshape(G, T, P).transpose(0, 2, 1),
        "w0": np.asarray(L0_gnn_weight), "wih_t": np.asarray(L0_gnn_w_ih).T, "whh_t": np.asarray(L0_gnn_w_hh).T,
        "bih": np.asarray(L0_gnn_b_ih).reshape(3, D).T, "bhh": np.asarray(L0_gnn_b_hh).reshape(3, D).T,
        "wq": pair_columns(np.asarray(L1_gnn_Wq)), "wk": pair_columns(np.asarray(L1_gnn_Wk)),
        "wv": np.asarray(L1_gnn_Wv), "wo": pair_rows(np.asarray(L1_gnn_Wo)),
        "bo": np.repeat(np.asarray(L1_gnn_bo)[None, :], P, axis=0), "kbias": kbias,
        "gat_w": np.stack([np.asarray(L2_gnn_W), np.asarray(L3_gnn_W)], axis=1),
        "gat_a": np.stack([a.T for a in gat_a], axis=1),
        "gat_arep": np.repeat(np.stack([a.T for a in gat_a], axis=1)[..., None], P, axis=3),
        "ident": np.eye(P, dtype=f32), "slot_sum": slot_sum, "slot_first": slot_first,
    }
    nc = bacc.Bacc("TRN2", target_bir_lowering=False, num_devices=1)
    feed, args = {}, []
    for name, a in arrays.items():
        feed["in_" + name] = np.ascontiguousarray(a)
        args.append(nc.dram_tensor("in_" + name, a.shape, mybir.dt.from_np(a.dtype), kind="ExternalInput").ap())
    out = nc.dram_tensor("out", (G, N, D), F32, kind="ExternalOutput").ap()
    build(nc, *args, out)
    return run(nc, [feed], core_ids=[0]).results[0]["out"]
```

```python
from contextlib import ExitStack

import concourse.bass as bass
from concourse import mybir

F32, BF16, I32 = mybir.dt.float32, mybir.dt.bfloat16, mybir.dt.int32
ACT = mybir.ActivationFunctionType
ALU = mybir.AluOpType

P = 128
G, N, D = 8, 1024, 128
T = N // P
HALF = N // 2
TH = T // 2
LAYERS = 3
HEADS, HD = 8, 16
PAIRS = HEADS // 2
SLOT = 32
Q_BLOCKS = (0, 0, 1, 0, 2, 1)
K_BLOCKS = (0, 1, 0, 2, 0, 1)
ROWS = HD * len(Q_BLOCKS)
PARTS = 3
SLOPE = 0.2
EPS = 1e-5
NO_EDGE = -float(2 ** 100)
LOWEST = -3.0e38
NEWTON = 4
ROWS_AHEAD = 3
STAGES = 4
PROBS = 16
OW = 132


def build(nc, x, adj, adj_t, nodemask, w0, wih_t, whh_t, bih, bhh, wq, wk, wv, wo, bo,
          gat_w, gat_a, gat_arep, ident, slot_sum, minus_part, out):
    with ExitStack() as ctx:
        def sb(name, shape, dt=F32):
            return ctx.enter_context(nc.sbuf_tensor(name, shape, dt))

        def sem(name):
            return ctx.enter_context(nc.semaphore(name))

        w0_s = sb("w0_s", [P, LAYERS, D])
        wih_s = sb("wih_s", [P, 3 * D])
        whh_s = sb("whh_s", [P, 3 * D])
        bih_s = sb("bih_s", [P, 3])
        bhh_s = sb("bhh_s", [P, 3])
        brz_s = sb("brz_s", [P, 3])
        wq_s = sb("wq_s", [P, D])
        wk_s = sb("wk_s", [P, D])
        wv_s = sb("wv_s", [P, D])
        wo_s = sb("wo_s", [P, PAIRS, 2, D])
        bo_s = sb("bo_s", [P, D])
        gw_s = sb("gw_s", [P, 2, D])
        ga_s = sb("ga_s", [P, 2, 2])
        garep_s = sb("garep_s", [P, 2, 2, P])
        ident_s = sb("ident_s", [P, P])
        identb_s = sb("identb_s", [P, P], BF16)
        slotsum_s = sb("slotsum_s", [P, P])
        minus_s = sb("minus_s", [P, 2])
        parts_s = sb("parts_s", [P, P], BF16)
        ones_s = sb("ones_s", [P, P])
        mask_s = sb("mask_s", [P, T])
        edge01 = sb("edge01", [P, T, N], BF16)
        noedge = sb("noedge", [P, T, N], BF16)
        noedge_t = sb("noedge_t", [P, T, N], BF16)
        stage = sb("stage", [P, STAGES, N], I32)
        xs = sb("xs", [P, T, D])
        xn = sb("xn", [P, T, D])
        hT = sb("hT", [P, N])
        stats = sb("stats", [P, T, 6])
        mv = sb("mv", [P, T, 2])
        nt1 = sb("nt1", [P, T]); nt2 = sb("nt2", [P, T]); nt3 = sb("nt3", [P, T])
        seed = sb("seed", [P, T], I32)
        m1 = sb("m1", [P, N], BF16); m2 = sb("m2", [P, N], BF16); m3 = sb("m3", [P, N], BF16)
        work = sb("work", [P, PROBS, HALF])
        q_rows = sb("q_rows", [P, HEADS, N], BF16)
        k_rows = sb("k_rows", [P, HEADS, N], BF16)
        qp = sb("qp", [P, PARTS, N], BF16)
        kp = sb("kp", [P, PARTS, N], BF16)
        vp = sb("vp", [P, T, HEADS, SLOT])
        rowmax = sb("rowmax", [P, PAIRS, 2 * T])
        maxrest = sb("maxrest", [P, 2, 2 * T])
        maxpart = sb("maxpart", [P, 2, PARTS * 2 * T], BF16)
        maxrow = sb("maxrow", [PARTS * 2 * T, 2, P], BF16)
        pvs = sb("pvs", [P, 2, HALF])
        rl = sb("rl", [P, 2, HALF])
        ctxn = sb("ctxn", [P, PAIRS, HALF])
        junk = sb("junk", [P, 2, N], BF16)
        wh = sb("wh", [P, T, OW])
        fcol = sb("fcol", [P, T, 2])
        mf2 = sb("mf2", [P, T]); gx = sb("gx", [P, T]); gm = sb("gm", [P, T])
        rinv = sb("rinv", [P, T])
        psum = ctx.enter_context(nc.psum_tensor("banks", [P, 8, HALF], F32))

        def two_banks(k):
            return psum[:, k:k + 2, :].rearrange("p a b -> p (a b)")

        workn = work[:, :, :].rearrange("p (a b) n -> p a (b n)", b=2)
        res1, aggT, rT, zT, tT, nT = (workn[:, k, :] for k in range(6))
        whT, mrow, diag = (q_rows[:, 2 * k:2 * k + 2, :].rearrange("p a n -> p (a n)").bitcast(F32) for k in range(3))
        f1part, f1rest = qp[:, 0, :], workn[:, 4, :]
        f1row = qp[:, 1, :]
        gup, gmin, gexp = (workn[:, k, :] for k in range(5, 8))

        weights_in = sem("weights_in")
        consts_ready, filled_s = sem("consts_ready"), sem("filled")
        pre_in, pre_done = sem("pre_in"), sem("pre_done")
        graph_done, cleared, resumed = sem("graph_done"), sem("cleared"), sem("resumed")
        names = ("x_in stored chain norm_ready turned hT_ready "
                 "msg_ready m1_ready res_ready m2_ready m3_ready agg_ready aggT_ready hn_ready r_ready "
                 "n_ready z_ready rT_ready zT_ready t_ready nT_ready h_ready back_ready "
                 "proj_ready part1_ready rest_ready part2_ready part3_ready rows_in maxpart_ready maxrow_ready "
                 "slot_ready slot_free v_psum v_ready score_ready prob_ready pv_done pair_saved "
                 "whT_psum wh_psum whT_ready wh_ready f2_ready fcol_ready f1_psum f1_part1 f1_rest f1_part2 f1_ready fcol_saved "
                 "diag_ready mrow_psum mrow_ready gscore_ready gsum_ready lrelu_ready shifted_ready gprob_ready "
                 "gpv_step gout_ready elu_in elu_out result_ready").split()
        S = {n: sem(n) for n in names}
        stage_in = [sem(f"stage_in{k}") for k in range(STAGES)]
        stage_used = [sem(f"stage_used{k}") for k in range(STAGES)]
        max_in = [sem(f"max_in{hp}") for hp in range(PAIRS)]
        per_graph = list(S.values()) + stage_in + stage_used + max_in

        def end_graph(eng, g):
            eng.drain().then_inc(graph_done, 1)
            eng.wait_ge(cleared, g + 1)
            eng.sem_inc(resumed, 1)

        def row_uses(hp):
            return [("row", hp, t, a) for t in range(T) for a in range(2)] + [("max", hp)]

        pair_uses = []
        for hp in range(PAIRS):
            uses = row_uses(hp + 1) if hp + 1 < PAIRS else []
            pair_uses.append(uses + ([("sum", hp - 1)] if hp >= 1 else []))
        slot_order = row_uses(0) + sum(pair_uses, []) + [("sum", PAIRS - 1), ("wo",)]
        slot_at = {u: n for n, u in enumerate(slot_order)}

        block = ctx.enter_context(nc.Block())

        loads = [(w0_s[:], w0.rearrange("l d e -> d l e")), (wih_s[:], wih_t), (whh_s[:], whh_t),
                 (bih_s[:], bih), (bhh_s[:], bhh), (wq_s[:], wq), (wk_s[:], wk), (wv_s[:], wv), (wo_s[:], wo),
                 (bo_s[:], bo), (gw_s[:], gat_w), (ga_s[:], gat_a),
                 (garep_s[:], gat_arep), (ident_s[:], ident), (slotsum_s[:], slot_sum), (minus_s[:], minus_part)]

        @block.sync
        def _(sp):
            for dst, src in loads:
                sp.dma_start(dst, src).then_inc(weights_in, 16)
            for t in range(T):
                if t >= STAGES and t % STAGES == 0:
                    sp.wait_ge(pre_done, t)
                sp.dma_start(stage[:, t % STAGES, :], adj[0, t * P:(t + 1) * P, :]).then_inc(pre_in, 16)
            sp.wait_ge(pre_done, T)
            with sp.Fori(0, G) as g:
                sp.dma_start(xs[:, :, :], x[bass.ds(g, 1)].rearrange("o (t p) d -> p (o t) d", p=P)).then_inc(S["x_in"], 16)
                sp.dma_start(mask_s[:, :], nodemask[bass.ds(g, 1)].rearrange("o p t -> p (o t)")).then_inc(S["x_in"], 16)
                nxt = (g + 1) % G

                def load(tiles):
                    for n in tiles:
                        k, t = n % STAGES, n % T
                        if n >= STAGES:
                            sp.wait_ge(stage_used[k], n // STAGES)
                        src = (adj[bass.ds(g, 1)], adj_t[bass.ds(g, 1)], adj[bass.ds(nxt, 1)])[n // T]
                        sp.dma_start(stage[:, k, :], src[:, t * P:(t + 1) * P, :].rearrange("o p n -> (o p) n")
                                     ).then_inc(stage_in[k], 16)

                load(range(2 * T + STAGES))
                for part, ready in enumerate(("part1_ready", "part2_ready", "part3_ready")):
                    for b, (blocks, src, dst) in enumerate(((Q_BLOCKS, qp, q_rows), (K_BLOCKS, kp, k_rows))):
                        sp.wait_ge(S[ready], b + 1)
                        for n, p in enumerate(blocks):
                            if p == part:
                                sp.dma_start(dst[n * HD:(n + 1) * HD, :, :], src[:, part, :]).then_inc(S["rows_in"], 16)
                for hp in range(PAIRS):
                    if hp == 2:
                        load(range(2 * T + STAGES, 3 * T))
                    sp.wait_ge(S["maxrow_ready"], hp + 1)
                    for p in range(PARTS):
                        sp.dma_start(q_rows[ROWS + p:ROWS + p + 1, 2 * hp:2 * hp + 2, :],
                                     maxrow[p * 2 * T:(p + 1) * 2 * T, hp % 2, :]).then_inc(max_in[hp], 16)
                sp.wait_ge(S["result_ready"], 1)
                sp.dma_start(out[bass.ds(g, 1)].rearrange("o (t p) d -> p (o t) d", p=P), xs[:, :, :]
                             ).then_inc(S["stored"], 16)
                sp.wait_ge(S["stored"], 16)
                end_graph(sp, g)

        @block.gpsimd
        def _(pool):
            filled = 0
            for dst, value in ((ones_s[:], 1.0), (vp[:, :, :, :], 0.0), (vp[:, :, :, HD:HD + 1], 1.0),
                               (k_rows[ROWS:ROWS + SLOT, :, :], -1.0), (wh[:, :, D:OW], 1.0),
                               (parts_s[:], 0.0), (parts_s[0:PARTS, :], 1.0)):
                if filled:
                    pool.wait_ge(filled_s, filled)
                pool.memset(dst, value).then_inc(filled_s, 1)
                filled += 1
            pool.wait_ge(filled_s, filled)
            pool.sem_inc(consts_ready, 1)
            pool.wait_ge(pre_done, T)
            with pool.Fori(0, G) as g:
                for n in range(2 * T):
                    k, t = n % STAGES, n % T
                    pool.wait_ge(stage_in[k], 16 * (n // STAGES + 1))
                    dst = (noedge, noedge_t)[n // T]
                    pool.tensor_scalar(dst[:, t, :], stage[:, k, :], 0.0, NO_EDGE, ALU.is_le, ALU.mult
                                       ).then_inc(stage_used[k], 1)
                pool.sem_inc(resumed, 1)
                pool.wait_ge(graph_done, 4 * (g + 1))
                pool.sem_inc(resumed, 1)
                for s in per_graph:
                    pool.sem_clear(s)
                pool.sem_inc(cleared, 1)
                pool.wait_ge(cleared, g + 1)
                pool.sem_inc(resumed, 1)

        def stage_tiles_done(eng, upto):
            for k in range(STAGES):
                eng.wait_ge(stage_used[k], (upto - k + STAGES - 1) // STAGES)

        @block.vector
        def _(dve):
            v = nc.vector
            dve.wait_ge(weights_in, 16 * len(loads))
            v.tensor_copy(identb_s[:], ident_s[:]).then_inc(consts_ready, 1)
            v.tensor_tensor(brz_s[:], bih_s[:], bhh_s[:], ALU.add).then_inc(consts_ready, 1)
            for t in range(T):
                if t % STAGES == 0:
                    dve.wait_ge(pre_in, 16 * (t + STAGES))
                v.tensor_scalar(edge01[:, t, :], stage[:, t % STAGES, :], 0.0, None, ALU.not_equal).then_inc(pre_done, 1)

            with dve.Fori(0, G) as g:
                links = [0]

                def link(ins):
                    links[0] += 1
                    ins.then_inc(S["chain"], 1)
                    dve.wait_ge(S["chain"], links[0])

                def normalise(k):
                    for t in range(T):
                        last = v.bn_stats(stats[:, t, :], xs[:, t, :])
                    link(last)
                    for t in range(T):
                        last = v.bn_aggr(mv[:, t, :], stats[:, t, :])
                    link(last)
                    link(v.tensor_scalar(nt1[:], mv[:, :, 1], EPS, None, ALU.add))
                    link(v.tensor_scalar(seed[:], nt1[:].bitcast(I32), 1, None, ALU.arith_shift_right))
                    link(v.tensor_scalar(seed[:], seed[:], -1.0, float(0x5F3759DF), ALU.mult, ALU.add))
                    y, y_next = seed[:].bitcast(F32), nt3[:]
                    for _ in range(NEWTON):
                        link(v.tensor_tensor(nt2[:], y, y, ALU.mult))
                        link(v.scalar_tensor_tensor(out=nt2[:], in0=nt2[:], scalar=-0.5, in1=nt1[:],
                                                    op0=ALU.mult, op1=ALU.mult))
                        link(v.scalar_tensor_tensor(out=y_next, in0=nt2[:], scalar=1.5, in1=y,
                                                    op0=ALU.add, op1=ALU.mult))
                        y, y_next = y_next, y
                    for t in range(T):
                        v.tensor_scalar(xn[:, t, :], xs[:, t, :], mv[:, t, 0:1], y[:, t:t + 1],
                                        ALU.subtract, ALU.mult).then_inc(S["norm_ready"], 1)

                dve.wait_ge(S["x_in"], 32)
                normalise(0)
                for l in range(LAYERS):
                    for h in range(2):
                        c = slice(h * HALF, (h + 1) * HALF)
                        dve.wait_ge(S["m1_ready"], 2 * l + h + 1)
                        v.tensor_tensor(res1[:, c], psum[:, h, :], m1[:, c], ALU.subtract).then_inc(S["res_ready"], 1)
                    for h in range(2):
                        c = slice(h * HALF, (h + 1) * HALF)
                        dve.wait_ge(S["m2_ready"], 2 * l + h + 1)
                        v.tensor_tensor(m3[:, c], res1[:, c], m2[:, c], ALU.subtract).then_inc(S["m3_ready"], 1)
                    for h in range(2):
                        c = slice(h * HALF, (h + 1) * HALF)
                        dve.wait_ge(S["rT_ready"], 2 * l + h + 1)
                        dve.wait_ge(S["hn_ready"], 2 * l + h + 1)
                        link(v.scalar_tensor_tensor(out=tT[:, c], in0=psum[:, h, :], scalar=bhh_s[:, 2:3], in1=rT[:, c],
                                                    op0=ALU.add, op1=ALU.mult))
                        dve.wait_ge(S["n_ready"], 2 * l + h + 1)
                        v.tensor_tensor(tT[:, c], psum[:, 2 + h, :], tT[:, c], ALU.add).then_inc(S["t_ready"], 1)
                    for h in range(2):
                        c = slice(h * HALF, (h + 1) * HALF)
                        dve.wait_ge(S["nT_ready"], 2 * l + h + 1)
                        link(v.tensor_tensor(tT[:, c], hT[:, c], nT[:, c], ALU.subtract))
                        dve.wait_ge(S["zT_ready"], 2 * l + h + 1)
                        link(v.tensor_tensor(tT[:, c], tT[:, c], zT[:, c], ALU.mult))
                        v.tensor_tensor(hT[:, c], tT[:, c], nT[:, c], ALU.add).then_inc(S["h_ready"], 1)
                for h in range(2):
                    dve.wait_ge(S["back_ready"], h + 1)
                    o = xs[:, h * TH:(h + 1) * TH, :].rearrange("p t d -> p (t d)")
                    last = v.tensor_tensor(o, psum[:, h, :], o, ALU.add)
                link(last)

                normalise(1)
                for h, (part, bank, scale) in enumerate(((qp, 0, HD ** -0.5), (kp, 2, 1.0))):
                    dve.wait_ge(S["part1_ready"], h + 1)
                    v.scalar_tensor_tensor(out=workn[:, h, :], in0=two_banks(bank), scalar=scale, in1=part[:, 0, :],
                                           op0=ALU.mult, op1=ALU.subtract).then_inc(S["rest_ready"], 1)
                for h, part in enumerate((qp, kp)):
                    dve.wait_ge(S["part2_ready"], h + 1)
                    v.tensor_tensor(part[:, 2, :], workn[:, h, :], part[:, 1, :], ALU.subtract).then_inc(S["part3_ready"], 1)

                def empty(use):
                    n, kind = slot_at[use], use[0]
                    bank = 2 * (n % 2)
                    dve.wait_ge(S["slot_ready"], n + 1)
                    if kind == "row":
                        _, hp, t, a = use
                        v.tensor_tensor_reduce(junk[:, n % 2, :], two_banks(bank), noedge[:, t, :], 1.0, LOWEST,
                                               ALU.add, ALU.max, rowmax[:, hp, a * T + t:a * T + t + 1]
                                               ).then_inc(S["slot_free"], 1)
                    elif kind == "max":
                        hp = use[1]
                        if hp >= 2:
                            dve.wait_ge(max_in[hp - 2], 16 * PARTS)
                        v.tensor_copy(maxrow[:, hp % 2, :], psum[0:PARTS * 2 * T, bank, :].bitcast(BF16)[:, 0:P]
                                      ).then_inc(S["slot_free"], 1)
                        dve.wait_ge(S["slot_free"], n + 1)
                        dve.sem_inc(S["maxrow_ready"], 1)
                    elif kind == "sum":
                        hp = use[1]
                        if hp >= 2:
                            dve.wait_ge(S["slot_free"], slot_at[("sum", hp - 2)] + 1)
                        link(v.reciprocal(rl[:, hp % 2, :], psum[:, bank, :]))
                        v.tensor_tensor(ctxn[:, hp, :], pvs[:, hp % 2, :], rl[:, hp % 2, :], ALU.mult).then_inc(S["slot_free"], 1)
                    elif kind == "wo":
                        for h in range(2):
                            o = xs[:, h * TH:(h + 1) * TH, :].rearrange("p t d -> p (t d)")
                            last = v.tensor_tensor(o, psum[:, bank + h, :], o, ALU.add)
                        link(last)

                def cut_maxima(hp):
                    c = [maxpart[:, hp % 2, p * 2 * T:(p + 1) * 2 * T] for p in range(PARTS)]
                    rest = maxrest[:, hp % 2, :]
                    dve.wait_ge(S["slot_free"], slot_at[("row", hp, T - 1, 1)] + 1)
                    link(v.tensor_copy(c[0], rowmax[:, hp, :]))
                    link(v.tensor_tensor(rest, rowmax[:, hp, :], c[0], ALU.subtract))
                    link(v.tensor_copy(c[1], rest))
                    v.tensor_tensor(c[2], rest, c[1], ALU.subtract).then_inc(S["maxpart_ready"], 1)

                stage_tiles_done(dve, T)
                for use in slot_order[:-2]:
                    if use[0] == "max":
                        cut_maxima(use[1])
                    empty(use)
                    if use[0] == "row" and use[1] == 2 and use[3]:
                        n = 2 * T + use[2]
                        dve.wait_ge(stage_in[n % STAGES], 16 * (n // STAGES + 1))
                        v.tensor_scalar(edge01[:, use[2], :], stage[:, n % STAGES, :], 0.0, None, ALU.not_equal
                                        ).then_inc(stage_used[n % STAGES], 1)
                xs_flat = xs[:, :, :].rearrange("p t d -> p (t d)")
                link(v.tensor_tensor(xs[:, :, :], xs[:, :, :], bo_s[:, None, :].to_broadcast([P, T, D]), ALU.add))
                empty(("sum", PAIRS - 1))
                empty(("wo",))

                for k in range(2):
                    normalise(2 + k)
                    for h in range(2):
                        dve.wait_ge(S["wh_psum"], 2 * k + h + 1)
                        v.tensor_copy(wh[:, h * TH:(h + 1) * TH, 0:D],
                                      psum[:, 2 + h, :].rearrange("p (t d) -> p t d", d=D)).then_inc(S["wh_ready"], 1)
                    dve.wait_ge(S["fcol_ready"], k + 1)
                    v.tensor_copy(fcol[:, :, :].rearrange("p t c -> p (t c)"), psum[:, 0, 0:2 * T]).then_inc(S["fcol_saved"], 1)
                    for h in range(2):
                        c = slice(h * HALF, (h + 1) * HALF)
                        dve.wait_ge(S["f1_part1"], 2 * k + h + 1)
                        v.scalar_tensor_tensor(out=f1rest[:, c], in0=f1part[:, c], scalar=minus_s[:, 0:1],
                                               in1=psum[:, (4, 7)[h], :], op0=ALU.mult, op1=ALU.add).then_inc(S["f1_rest"], 1)
                    for h in range(2):
                        c = slice(h * HALF, (h + 1) * HALF)
                        dve.wait_ge(S["f1_part2"], 2 * k + h + 1)
                        v.scalar_tensor_tensor(out=f1row[:, c], in0=f1part[:, c], scalar=minus_s[:, 1:2],
                                               in1=f1rest[:, c], op0=ALU.mult, op1=ALU.add).then_inc(S["f1_ready"], 1)
                    dve.wait_ge(S["f2_ready"], k + 1)
                    for t in range(T):
                        if t >= 2:
                            dve.wait_ge(S["chain"], links[0] - 1)
                        v.tensor_tensor_reduce(junk[:, t % 2, :], two_banks(5), noedge[:, t, :], 1.0, LOWEST,
                                               ALU.add, ALU.max, mf2[:, t:t + 1]).then_inc(S["chain"], 1)
                        links[0] += 1
                    dve.wait_ge(S["chain"], links[0])
                    dve.wait_ge(S["fcol_saved"], k + 1)
                    link(v.tensor_tensor(gx[:], mf2[:], fcol[:, :, 0], ALU.add))
                    link(v.scalar_tensor_tensor(out=gm[:], in0=gx[:], scalar=SLOPE, in1=gx[:], op0=ALU.mult, op1=ALU.max))
                    v.tensor_tensor(diag.rearrange("p (t n) -> p t n", t=T), ident_s[:, None, :].to_broadcast([P, T, P]),
                                    gm[:, :, None].to_broadcast([P, T, P]), ALU.mult).then_inc(S["diag_ready"], 1)
                    dve.wait_ge(S["mrow_ready"], 2 * (k + 1))

                    def lrelu(t):
                        dve.wait_ge(S["gsum_ready"], k * T + t + 1)
                        y = workn[:, t % 2, :]
                        v.scalar_tensor_tensor(out=y, in0=y, scalar=SLOPE, in1=y, op0=ALU.mult, op1=ALU.max
                                               ).then_inc(S["lrelu_ready"], 1)

                    lrelu(0)
                    for t in range(T):
                        if t + 1 < T:
                            lrelu(t + 1)
                        dve.wait_ge(S["lrelu_ready"], k * T + t + 1)
                        y = workn[:, t % 2, :]
                        v.tensor_tensor(y, y, mrow, ALU.subtract).then_inc(S["shifted_ready"], 1)
                    dve.wait_ge(S["gpv_step"], T * (k + 1))
                    for b in range(3):
                        nb = min(3, T - 3 * b)
                        o = psum[:, 5 + b, 0:nb * OW].rearrange("p (t c) -> p t c", c=OW)
                        last = v.reciprocal(rinv[:, 3 * b:3 * b + nb], o[:, :, D])
                    link(last)
                    if k == 0:
                        link(v.tensor_tensor(rinv[:], rinv[:], mask_s[:], ALU.mult))
                    up = gup.rearrange("p (t d) -> p t d", t=T)
                    for b in range(3):
                        nb = min(3, T - 3 * b)
                        o = psum[:, 5 + b, 0:nb * OW].rearrange("p (t c) -> p t c", c=OW)
                        last = v.tensor_tensor(up[:, 3 * b:3 * b + nb, :], o[:, :, 0:D],
                                               rinv[:, 3 * b:3 * b + nb, None].to_broadcast([P, nb, D]), ALU.mult)
                    last.then_inc(S["gout_ready"], 1)
                    dve.wait_ge(S["gout_ready"], k + 1)
                    if k == 0:
                        v.tensor_scalar(gmin, gup, 0.0, None, ALU.min).then_inc(S["elu_in"], 1)
                        link(v.scalar_tensor_tensor(out=xs_flat, in0=gup, scalar=0.0, in1=xs_flat, op0=ALU.max, op1=ALU.add))
                        dve.wait_ge(S["elu_out"], 1)
                        link(v.scalar_tensor_tensor(out=xs_flat, in0=gexp, scalar=-1.0, in1=xs_flat, op0=ALU.add, op1=ALU.add))
                    else:
                        v.scalar_tensor_tensor(out=xs_flat, in0=gup, scalar=0.0, in1=xs_flat, op0=ALU.max, op1=ALU.add
                                               ).then_inc(S["result_ready"], 1)
                end_graph(dve, g)

        @block.scalar
        def _(act):
            a = nc.scalar

            def turn_in(k):
                for h in range(2):
                    act.wait_ge(S["turned"], 2 * k + h + 1)
                    a.activation(hT[:, h * HALF:(h + 1) * HALF], psum[:, h, :], ACT.Relu).then_inc(S["hT_ready"], 1)

            act.wait_ge(consts_ready, 3)
            with act.Fori(0, G) as g:
                turn_in(0)
                for l in range(LAYERS):
                    for h in range(2):
                        c = slice(h * HALF, (h + 1) * HALF)
                        act.wait_ge(S["msg_ready"], 2 * l + h + 1)
                        a.copy(m1[:, c], psum[:, h, :]).then_inc(S["m1_ready"], 1)
                    for h in range(2):
                        c = slice(h * HALF, (h + 1) * HALF)
                        act.wait_ge(S["res_ready"], 2 * l + h + 1)
                        a.copy(m2[:, c], res1[:, c]).then_inc(S["m2_ready"], 1)
                    for h in range(2):
                        c = slice(h * HALF, (h + 1) * HALF)
                        act.wait_ge(S["agg_ready"], 2 * l + h + 1)
                        a.copy(aggT[:, c], psum[:, 2 + h, :]).then_inc(S["aggT_ready"], 1)
                    for h in range(2):
                        c = slice(h * HALF, (h + 1) * HALF)
                        act.wait_ge(S["r_ready"], 2 * l + h + 1)
                        a.activation(rT[:, c], psum[:, 4 + h, :], ACT.Sigmoid, bias=brz_s[:, 0:1]).then_inc(S["rT_ready"], 1)
                        act.wait_ge(S["z_ready"], 2 * l + h + 1)
                        a.activation(zT[:, c], psum[:, 6 + h, :], ACT.Sigmoid, bias=brz_s[:, 1:2]).then_inc(S["zT_ready"], 1)
                    for h in range(2):
                        c = slice(h * HALF, (h + 1) * HALF)
                        act.wait_ge(S["t_ready"], 2 * l + h + 1)
                        a.activation(nT[:, c], tT[:, c], ACT.Tanh, bias=bih_s[:, 2:3]).then_inc(S["nT_ready"], 1)

                turn_in(1)
                for part, bank, h, scale in ((qp, 0, 0, HD ** -0.5), (kp, 2, 1, 1.0)):
                    act.wait_ge(S["proj_ready"], h + 1)
                    a.activation(part[:, 0, :], two_banks(bank), ACT.Copy, scale=scale).then_inc(S["part1_ready"], 1)
                for h, part in enumerate((qp, kp)):
                    act.wait_ge(S["rest_ready"], h + 1)
                    a.copy(part[:, 1, :], workn[:, h, :]).then_inc(S["part2_ready"], 1)
                act.wait_ge(S["v_psum"], 2)
                a.copy(vp[:, :, :, 0:HD], two_banks(4).rearrange("p (t h d) -> p t h d", t=T, h=HEADS)).then_inc(S["v_ready"], 1)
                for hp in range(PAIRS):
                    for u in range(4 * T):
                        n = 4 * T * hp + u
                        act.wait_ge(S["score_ready"], n + 1)
                        if n >= PROBS:
                            act.wait_ge(S["pv_done"], (n - PROBS) // 4 + 1)
                        a.activation(work[:, n % PROBS, :], psum[:, 4 + n % 3, :], ACT.Exp).then_inc(S["prob_ready"], 1)
                        if hp >= 1 and u == 3:
                            act.wait_ge(S["pv_done"], T * hp)
                            if hp >= 3:
                                act.wait_ge(S["slot_free"], slot_at[("sum", hp - 3)] + 1)
                            a.copy(pvs[:, (hp - 1) % 2, :], psum[:, 7, :]).then_inc(S["pair_saved"], 1)
                act.wait_ge(S["pv_done"], T * PAIRS)
                act.wait_ge(S["slot_free"], slot_at[("sum", PAIRS - 3)] + 1)
                a.copy(pvs[:, (PAIRS - 1) % 2, :], psum[:, 7, :]).then_inc(S["pair_saved"], 1)

                for k in range(2):
                    turn_in(2 + k)
                    for h in range(2):
                        act.wait_ge(S["whT_psum"], 2 * k + h + 1)
                        a.copy(whT[:, h * HALF:(h + 1) * HALF], psum[:, h, :]).then_inc(S["whT_ready"], 1)
                    for h in range(2):
                        act.wait_ge(S["f1_psum"], 2 * k + h + 1)
                        a.copy(f1part[:, h * HALF:(h + 1) * HALF], psum[:, (4, 7)[h], :]).then_inc(S["f1_part1"], 1)
                    for h in range(2):
                        act.wait_ge(S["f1_rest"], 2 * k + h + 1)
                        a.copy(f1part[:, h * HALF:(h + 1) * HALF], f1rest[:, h * HALF:(h + 1) * HALF]).then_inc(S["f1_part2"], 1)

                    def add_f2(t):
                        act.wait_ge(S["gscore_ready"], k * T + t + 1)
                        act.wait_ge(S["fcol_saved"], k + 1)
                        if t >= 2:
                            act.wait_ge(S["gprob_ready"], k * T + t - 1)
                        a.activation(workn[:, t % 2, :], two_banks(1 + 2 * (t % 2)), ACT.Identity,
                                     bias=fcol[:, t, 1:2]).then_inc(S["gsum_ready"], 1)

                    add_f2(0)
                    for h in range(2):
                        act.wait_ge(S["mrow_psum"], 2 * k + h + 1)
                        a.copy(mrow[:, h * HALF:(h + 1) * HALF], psum[:, (0, 7)[h], :]).then_inc(S["mrow_ready"], 1)
                    add_f2(1)
                    for t in range(T):
                        act.wait_ge(S["shifted_ready"], k * T + t + 1)
                        if t >= 2:
                            act.wait_ge(S["gpv_step"], k * T + t - 1)
                        a.activation(workn[:, 2 + t % 2, :], workn[:, t % 2, :], ACT.Exp).then_inc(S["gprob_ready"], 1)
                        if t + 2 < T:
                            add_f2(t + 2)
                    if k == 0:
                        act.wait_ge(S["elu_in"], 1)
                        a.activation(gexp, gmin, ACT.Exp).then_inc(S["elu_out"], 1)
                end_graph(act, g)

        @block.tensor
        def _(pe):
            mm = nc.tensor.matmul

            def turn_out(k):
                for h in range(2):
                    pe.wait_ge(S["norm_ready"], k * T + (h + 1) * TH)
                    for t in range(TH):
                        last = nc.tensor.transpose(psum[:, h, t * P:(t + 1) * P], xn[:, h * TH + t, :], ident_s[:])
                    last.then_inc(S["turned"], 1)

            pe.wait_ge(consts_ready, 3)
            with pe.Fori(0, G) as g:
                turn_out(0)
                for l in range(LAYERS):
                    for h in range(2):
                        if l == 0:
                            pe.wait_ge(S["hT_ready"], h + 1)
                            if h == 0:
                                pe.wait_ge(S["hT_ready"], 2)
                        else:
                            pe.wait_ge(S["h_ready"], 2 * (l - 1) + h + 1)
                        for t in range(TH):
                            last = mm(psum[:, h, t * P:(t + 1) * P], hT[:, (h * TH + t) * P:(h * TH + t + 1) * P],
                                      w0_s[:, l, :], start=True, stop=True)
                        last.then_inc(S["msg_ready"], 1)
                    for gate in range(2):
                        for h in range(2):
                            mm(psum[:, 4 + 2 * gate + h, :], whh_s[:, gate * D:(gate + 1) * D],
                               hT[:, h * HALF:(h + 1) * HALF], start=True, stop=False)
                    for part, (m, ready) in enumerate(((m1, "m1_ready"), (m2, "m2_ready"), (m3, "m3_ready"))):
                        for s in range(T):
                            if s % TH == 0:
                                pe.wait_ge(S[ready], 2 * l + s // TH + 1)
                            for h in range(2):
                                last = mm(psum[:, 2 + h, :], m[:, s * P:(s + 1) * P], edge01[:, s, h * HALF:(h + 1) * HALF],
                                          start=(part == 0 and s == 0), stop=(part == 2 and s == T - 1))
                                if part == 2 and s == T - 1:
                                    last.then_inc(S["agg_ready"], 1)
                    for h in range(2):
                        pe.wait_ge(S["res_ready"], 2 * l + h + 1)
                        mm(psum[:, h, :], whh_s[:, 2 * D:3 * D], hT[:, h * HALF:(h + 1) * HALF],
                           start=True, stop=True).then_inc(S["hn_ready"], 1)
                    for h in range(2):
                        c = slice(h * HALF, (h + 1) * HALF)
                        pe.wait_ge(S["aggT_ready"], 2 * l + h + 1)
                        mm(psum[:, 4 + h, :], wih_s[:, 0:D], aggT[:, c], start=False, stop=True).then_inc(S["r_ready"], 1)
                        mm(psum[:, 2 + h, :], wih_s[:, 2 * D:3 * D], aggT[:, c], start=True, stop=True).then_inc(S["n_ready"], 1)
                        mm(psum[:, 6 + h, :], wih_s[:, D:2 * D], aggT[:, c], start=False, stop=True).then_inc(S["z_ready"], 1)
                for h in range(2):
                    pe.wait_ge(S["h_ready"], 2 * (LAYERS - 1) + h + 1)
                    for t in range(TH):
                        last = nc.tensor.transpose(psum[:, h, t * P:(t + 1) * P],
                                                   hT[:, (h * TH + t) * P:(h * TH + t + 1) * P], ident_s[:])
                    last.then_inc(S["back_ready"], 1)

                turn_out(1)
                pe.wait_ge(S["hT_ready"], 4)

                def fill(use):
                    n, kind = slot_at[use], use[0]
                    bank = 2 * (n % 2)
                    if n >= 2:
                        pe.wait_ge(S["slot_free"], n - 1)
                    if kind == "row":
                        _, hp, t, a = use
                        for h in range(2):
                            last = mm(psum[:, bank + h, :], q_rows[0:ROWS, 2 * hp + a, t * P:(t + 1) * P],
                                      k_rows[0:ROWS, 2 * hp + a, h * HALF:(h + 1) * HALF], start=True, stop=True)
                    elif kind == "max":
                        pe.wait_ge(S["maxpart_ready"], use[1] + 1)
                        last = nc.tensor.transpose(psum[0:PARTS * 2 * T, bank, :].bitcast(BF16)[:, 0:P],
                                                   maxpart[:, use[1] % 2, :], identb_s[:])
                    elif kind == "sum":
                        pe.wait_ge(S["pair_saved"], use[1] + 1)
                        last = mm(psum[:, bank, :], slotsum_s[:], pvs[:, use[1] % 2, :], start=True, stop=True)
                    elif kind == "wo":
                        pe.wait_ge(S["slot_free"], n)
                        for t in range(T):
                            c = slice(t % TH * P, (t % TH + 1) * P)
                            for hp in range(PAIRS):
                                last = mm(psum[:, bank + t // TH, c], ctxn[:, hp, c], wo_s[:, hp, t // TH, :],
                                          start=(hp == 0), stop=(hp == PAIRS - 1))
                    last.then_inc(S["slot_ready"], 1)

                def values():
                    for h in range(2):
                        for t in range(TH):
                            last = mm(psum[:, 4 + h, t * P:(t + 1) * P], hT[:, (h * TH + t) * P:(h * TH + t + 1) * P],
                                      wv_s[:], start=True, stop=True)
                        last.then_inc(S["v_psum"], 1)

                def scores(hp, kt):
                    for j in range(4):
                        n = 4 * (T * hp + kt) + j
                        if n >= 3:
                            pe.wait_ge(S["prob_ready"], n - 2)
                        mm(psum[:, 4 + n % 3, :], identb_s[:], noedge_t[:, kt, (j % 2) * HALF:(j % 2 + 1) * HALF],
                           start=True, stop=False)
                        mm(psum[:, 4 + n % 3, :], k_rows[0:ROWS + PARTS, 2 * hp + j // 2, kt * P:(kt + 1) * P],
                           q_rows[0:ROWS + PARTS, 2 * hp + j // 2, (j % 2) * HALF:(j % 2 + 1) * HALF],
                           start=False, stop=True).then_inc(S["score_ready"], 1)

                def context(hp, kt):
                    n = T * hp + kt
                    pe.wait_ge(S["prob_ready"], 4 * n + 4)
                    if kt == 0 and hp >= 1:
                        pe.wait_ge(S["pair_saved"], hp)
                    for j in range(4):
                        last = mm(psum[SLOT * j:SLOT * (j + 1), 7, :], vp[:, kt, 2 * hp + j // 2, :],
                                  work[:, (4 * n + j) % PROBS, :], start=(kt == 0), stop=(kt == T - 1))
                    last.then_inc(S["pv_done"], 1)

                for b, w in enumerate((wq_s, wk_s)):
                    for h in range(2):
                        last = mm(psum[:, 2 * b + h, :], w[:], hT[:, h * HALF:(h + 1) * HALF], start=True, stop=True)
                    last.then_inc(S["proj_ready"], 1)
                values()
                pe.wait_ge(S["rest_ready"], 2)
                pe.wait_ge(S["rows_in"], 16 * (len(Q_BLOCKS) + len(K_BLOCKS)))
                for use in row_uses(0):
                    fill(use)
                pe.wait_ge(S["v_ready"], 1)
                stage_tiles_done(pe, 2 * T)
                for hp in range(PAIRS):
                    uses = list(pair_uses[hp])
                    while len(uses) > 2 * T + 2 - ROWS_AHEAD:
                        fill(uses.pop(0))
                    pe.wait_ge(max_in[hp], 16 * PARTS)
                    for kt in range(T):
                        scores(hp, kt)
                        for _ in range(ROWS_AHEAD):
                            if uses and (uses[0][0] != "sum" or kt > 2):
                                fill(uses.pop(0))
                        if kt:
                            context(hp, kt - 1)
                    context(hp, T - 1)
                    for use in uses:
                        fill(use)
                fill(("sum", PAIRS - 1))
                fill(("wo",))

                for k in range(2):
                    turn_out(2 + k)
                    pe.wait_ge(S["hT_ready"], 2 * (3 + k))
                    for h in range(2):
                        mm(psum[:, h, :], gw_s[:, k, :], hT[:, h * HALF:(h + 1) * HALF],
                           start=True, stop=True).then_inc(S["whT_psum"], 1)
                    for h in range(2):
                        for t in range(TH):
                            last = mm(psum[:, 2 + h, t * P:(t + 1) * P], hT[:, (h * TH + t) * P:(h * TH + t + 1) * P],
                                      gw_s[:, k, :], start=True, stop=True)
                        last.then_inc(S["wh_psum"], 1)
                    pe.wait_ge(S["whT_ready"], 2 * (k + 1))
                    for h in range(2):
                        last = mm(psum[:, 5 + h, :], garep_s[:, k, 1, :], whT[:, h * HALF:(h + 1) * HALF], start=True, stop=True)
                    last.then_inc(S["f2_ready"], 1)
                    for t in range(T):
                        last = mm(psum[:, 0, 2 * t:2 * t + 2], whT[:, t * P:(t + 1) * P], ga_s[:, k, :], start=True, stop=True)
                    last.then_inc(S["fcol_ready"], 1)
                    for h in range(2):
                        mm(psum[:, (4, 7)[h], :], garep_s[:, k, 0, :], whT[:, h * HALF:(h + 1) * HALF],
                           start=True, stop=True).then_inc(S["f1_psum"], 1)
                    pe.wait_ge(S["wh_ready"], 2 * (k + 1))
                    pe.wait_ge(S["f1_ready"], 2 * (k + 1))

                    def gat_scores(t):
                        if t >= 2:
                            pe.wait_ge(S["gsum_ready"], k * T + t - 1)
                        b = 1 + 2 * (t % 2)
                        for h in range(2):
                            mm(psum[:, b + h, :], identb_s[:], noedge_t[:, t, h * HALF:(h + 1) * HALF],
                               start=True, stop=False)
                        for h in range(2):
                            last = mm(psum[:, b + h, :], parts_s[:], f1row[:, h * HALF:(h + 1) * HALF],
                                      start=False, stop=True)
                        last.then_inc(S["gscore_ready"], 1)

                    gat_scores(0)
                    gat_scores(1)
                    pe.wait_ge(S["diag_ready"], k + 1)
                    pe.wait_ge(S["fcol_saved"], k + 1)
                    for h in range(2):
                        mm(psum[:, (0, 7)[h], :], ones_s[:], diag[:, h * HALF:(h + 1) * HALF],
                           start=True, stop=True).then_inc(S["mrow_psum"], 1)
                    pe.wait_ge(S["mrow_ready"], 2 * (k + 1))
                    for t in range(T):
                        pe.wait_ge(S["gprob_ready"], k * T + t + 1)
                        for i in range(T):
                            last = mm(psum[:, 5 + i // 3, (i % 3) * OW:(i % 3) * OW + D + 1],
                                      workn[:, 2 + t % 2, i * P:(i + 1) * P], wh[:, t, 0:D + 1],
                                      start=(t == 0 and i % 3 == 0), stop=(t == T - 1), skip_group_check=True)
                        last.then_inc(S["gpv_step"], 1)
                        if t + 2 < T:
                            gat_scores(t + 2)
                end_graph(pe, g)


def kernel(x, adj, nodemask, L0_gnn_weight, L0_gnn_w_ih, L0_gnn_w_hh, L0_gnn_b_ih, L0_gnn_b_hh,
           L1_gnn_Wq, L1_gnn_Wk, L1_gnn_Wv, L1_gnn_Wo, L1_gnn_bo, L2_gnn_W, L2_gnn_a, L3_gnn_W, L3_gnn_a):
    import numpy as np
    import concourse.bacc as bacc
    from concourse.bass_utils import run_bass_kernel_spmd as run

    def by_row(w):
        return w.reshape(D, HEADS, HD).transpose(0, 2, 1).reshape(D, D)

    def pair_rows(w):
        o = np.zeros((PAIRS, 2, 2, 2, SLOT, D), w.dtype)
        rows = w.reshape(PAIRS, 2, HD, D)
        for b in range(2):
            o[:, b, :, b, :HD] = rows
        return o.reshape(PAIRS, 2, P, D).transpose(2, 0, 1, 3)

    f32 = np.float32
    row = np.arange(P)
    minus_part = -np.stack([(row >= 1) & (row < PARTS), row == PARTS - 1], axis=1).astype(f32)
    slot_sum = ((row[:, None] % SLOT == HD) & (row[:, None] // SLOT == row[None, :] // SLOT)).astype(f32)
    x, adj, nodemask = np.asarray(x), np.asarray(adj), np.asarray(nodemask)
    gat_a = [np.asarray(a).reshape(2, D) for a in (L2_gnn_a, L3_gnn_a)]
    arrays = {
        "x": x, "adj": adj, "adj_t": adj.transpose(0, 2, 1),
        "nodemask": nodemask.reshape(G, T, P).transpose(0, 2, 1),
        "w0": np.asarray(L0_gnn_weight), "wih_t": np.asarray(L0_gnn_w_ih).T, "whh_t": np.asarray(L0_gnn_w_hh).T,
        "bih": np.asarray(L0_gnn_b_ih).reshape(3, D).T, "bhh": np.asarray(L0_gnn_b_hh).reshape(3, D).T,
        "wq": by_row(np.asarray(L1_gnn_Wq)), "wk": by_row(np.asarray(L1_gnn_Wk)),
        "wv": np.asarray(L1_gnn_Wv), "wo": pair_rows(np.asarray(L1_gnn_Wo)),
        "bo": np.repeat(np.asarray(L1_gnn_bo)[None, :], P, axis=0),
        "gat_w": np.stack([np.asarray(L2_gnn_W), np.asarray(L3_gnn_W)], axis=1),
        "gat_a": np.stack([a.T for a in gat_a], axis=1),
        "gat_arep": np.repeat(np.stack([a.T for a in gat_a], axis=1)[..., None], P, axis=3),
        "ident": np.eye(P, dtype=f32), "slot_sum": slot_sum, "minus_part": minus_part,
    }
    nc = bacc.Bacc("TRN2", target_bir_lowering=False, num_devices=1)
    feed, args = {}, []
    for name, a in arrays.items():
        feed["in_" + name] = np.ascontiguousarray(a)
        args.append(nc.dram_tensor("in_" + name, a.shape, mybir.dt.from_np(a.dtype), kind="ExternalInput").ap())
    out = nc.dram_tensor("out", (G, N, D), F32, kind="ExternalOutput").ap()
    build(nc, *args, out)
    return run(nc, [feed], core_ids=[0]).results[0]["out"]
```

```python
from contextlib import ExitStack

import concourse.bass as bass
from concourse import mybir

F32, BF16, I32 = mybir.dt.float32, mybir.dt.bfloat16, mybir.dt.int32
ACT = mybir.ActivationFunctionType
ALU = mybir.AluOpType

P = 128
G, N, D = 8, 1024, 128
T = N // P
HALF = N // 2
TH = T // 2
LAYERS = 3
HEADS, HD = 8, 16
PAIRS = HEADS // 2
SLOT = 32
Q_BLOCKS = (0, 0, 1, 0, 2, 1)
K_BLOCKS = (0, 1, 0, 2, 0, 1)
ROWS = HD * len(Q_BLOCKS)
PARTS = 3
SLOPE = 0.2
EPS = 1e-5
NO_EDGE = -float(2 ** 100)
LOWEST = -3.0e38
NEWTON = 3
YBUFS, GBUFS = 4, 3
STAGES = 4
PROBS = 16
OW = 132


def build(nc, x, adj, adj_t, nodemask, w0, wih_t, whh_t, bih, bhh, wq, wk, wv, wo, bo,
          gat_w, gat_wt, gat_a, gat_arep, ident, slot_sum, minus_part, out):
    with ExitStack() as ctx:
        def sb(name, shape, dt=F32):
            return ctx.enter_context(nc.sbuf_tensor(name, shape, dt))

        def sem(name):
            return ctx.enter_context(nc.semaphore(name))

        w0_s = sb("w0_s", [P, LAYERS, D])
        wih_s = sb("wih_s", [P, 3 * D])
        whh_s = sb("whh_s", [P, 3 * D])
        bih_s = sb("bih_s", [P, 3])
        bhh_s = sb("bhh_s", [P, 3])
        brz_s = sb("brz_s", [P, 3])
        wq_s = sb("wq_s", [P, D])
        wk_s = sb("wk_s", [P, D])
        wv_s = sb("wv_s", [P, D])
        wo_s = sb("wo_s", [P, PAIRS, 2, D])
        bo_s = sb("bo_s", [P, D])
        gw_s = sb("gw_s", [P, 2, D])
        ga_s = sb("ga_s", [P, 2, 2])
        wa_s = sb("wa_s", [P, 2, 2])
        warep_s = sb("warep_s", [P, 2, 2, P])
        ident_s = sb("ident_s", [P, P])
        identb_s = sb("identb_s", [P, P], BF16)
        slotsum_s = sb("slotsum_s", [P, P])
        minus_s = sb("minus_s", [P, 2])
        minusdiag_s = sb("minusdiag_s", [P, 2, P], BF16)
        parts_s = sb("parts_s", [P, P], BF16)
        ones_s = sb("ones_s", [P, P])
        mask_s = sb("mask_s", [P, T])
        edge01 = sb("edge01", [P, T, N], BF16)
        noedge = sb("noedge", [P, T, N], BF16)
        noedge_t = sb("noedge_t", [P, T, N], BF16)
        stage = sb("stage", [P, STAGES, N], I32)
        xs = sb("xs", [P, T, D])
        xn = sb("xn", [P, T, D])
        hT = sb("hT", [P, N])
        stats = sb("stats", [P, T, 6])
        mv = sb("mv", [P, T, 2])
        nt1 = sb("nt1", [P, T]); nt2 = sb("nt2", [P, T]); nt3 = sb("nt3", [P, T])
        seed = sb("seed", [P, T], I32)
        msg_parts = sb("msg_parts", [P, 3, N], BF16)
        work = sb("work", [P, PROBS, HALF])
        q_rows = sb("q_rows", [P, HEADS, N], BF16)
        k_rows = sb("k_rows", [P, HEADS, N], BF16)
        qp = sb("qp", [P, PARTS, N], BF16)
        kp = sb("kp", [P, PARTS, N], BF16)
        vp = sb("vp", [P, T, HEADS, SLOT])
        rowmax = sb("rowmax", [P, PAIRS, 2 * T])
        maxrest = sb("maxrest", [P, 2, 2 * T])
        maxpart = sb("maxpart", [P, 2, PARTS * 2 * T], BF16)
        maxrow = sb("maxrow", [PARTS * 2 * T, 2, P], BF16)
        pvs = sb("pvs", [P, 2, HALF])
        rl = sb("rl", [P, HALF])
        ctxn = sb("ctxn", [P, PAIRS, HALF])
        junk = sb("junk", [P, 2, N], BF16)
        wh = sb("wh", [P, T, OW])
        fcol = sb("fcol", [P, T, 2])
        mf2 = sb("mf2", [P, T]); gx = sb("gx", [P, T]); gm = sb("gm", [P, T])
        rinv = sb("rinv", [P, T])
        psum = ctx.enter_context(nc.psum_tensor("banks", [P, 8, HALF], F32))

        halves = (slice(0, HALF), slice(HALF, N))
        quarters = (slice(0, HALF // 2), slice(HALF // 2, HALF))

        def two_banks(k):
            return psum[:, k:k + 2, :].rearrange("p a b -> p (a b)")

        workn = work[:, :, :].rearrange("p (a b) n -> p a (b n)", b=2)
        m1, m2, m3 = (msg_parts[:, p, :] for p in range(3))
        garep_s = work[:, 0, :].rearrange("p (k c n) -> p k c n", k=2, c=2)
        gwt_s = work[:, 1, 0:2 * D].rearrange("p (k d) -> p k d", k=2)
        xnext = msg_parts[:, 0:2, :].rearrange("p a n -> p (a n)").bitcast(F32).rearrange("p (t d) -> p t d", t=T)
        result = ctxn[:, 0:2, :].rearrange("p a n -> p (a n)")
        res1, aggT, rT, zT, tT, nT = (workn[:, k, :] for k in range(6))
        mrow, diag = (q_rows[:, 2 * k:2 * k + 2, :].rearrange("p a n -> p (a n)").bitcast(F32) for k in range(2))
        f1part = qp[:, 0:2, :]
        f1row = qp[:, 2, :]
        gup, gmin, gexp = (workn[:, k, :] for k in range(5, 8))

        weights_in = sem("weights_in")
        consts_ready, filled_s, folded = sem("consts_ready"), sem("filled"), sem("folded")
        CONSTS = 9
        pre_in, pre_done = sem("pre_in"), sem("pre_done")
        x_in, stored = sem("x_in"), sem("stored")
        pre_chain, normed = sem("pre_chain"), sem("normed")
        graph_done, cleared, resumed = sem("graph_done"), sem("cleared"), sem("resumed")
        names = ("chain norm_ready turned hT_ready "
                 "msg_ready m1_ready res_ready m2_ready m3_ready agg_ready aggT_ready hn_ready r_ready "
                 "n_ready z_ready rT_ready zT_ready t_ready nT_ready h_ready back_ready "
                 "proj_ready part1_ready rest_ready part2_ready part3_ready rows0_in rows_in maxpart_ready maxrow_ready "
                 "slot_ready slot_free v_psum v_ready score_ready prob_ready pv_done pair_saved "
                 "wh_psum wh_ready f2_ready fcol_ready f1_psum f1_part f1_ready fcol_saved "
                 "diag_ready mrow_psum mrow_ready gscore_ready gsum_ready lrelu_ready shifted_ready gprob_ready "
                 "gpv_step gout_ready elu_in elu_out result_ready mask_in x_saved divided").split()
        S = {n: sem(n) for n in names}
        stage_in = [sem(f"stage_in{k}") for k in range(STAGES)]
        stage_used = [sem(f"stage_used{k}") for k in range(STAGES)]
        max_in = [sem(f"max_in{hp}") for hp in range(PAIRS)]
        per_graph = list(S.values()) + stage_in + stage_used + max_in

        ENGINES = 5
        SP_CLEARS, POOL_CLEARS, DVE_CLEARS, ACT_CLEARS, PE_CLEARS = (per_graph[e::ENGINES] for e in range(ENGINES))

        def end_graph(eng, g, own):
            eng.drain().then_inc(graph_done, 1)
            eng.wait_ge(graph_done, ENGINES * (g + 1))
            eng.sem_inc(resumed, 1)
            for s in own:
                eng.sem_clear(s)
            eng.sem_inc(cleared, 1)
            eng.wait_ge(cleared, ENGINES * (g + 1))
            eng.sem_inc(resumed, 1)

        def row_uses(hp):
            return [("row", hp, t, a) for t in range(T) for a in range(2)] + [("max", hp)]

        pair_uses = []
        for hp in range(PAIRS):
            uses = row_uses(hp + 1) if hp + 1 < PAIRS else []
            pair_uses.append(uses + ([("sum", hp - 1)] if hp >= 1 else []))
        slot_order = row_uses(0) + sum(pair_uses, []) + [("sum", PAIRS - 1), ("wo",)]
        convert_after = ([("row", 1, t, 1) for t in range(1, T, 2)]
                         + [("row", hp, t, 1) for hp in (2, 3) for t in (T // 2 - 1, T - 2)])
        slot_at = {u: n for n, u in enumerate(slot_order)}

        block = ctx.enter_context(nc.Block())

        loads = [(w0_s[:], w0.rearrange("l d e -> d l e")), (wih_s[:], wih_t), (whh_s[:], whh_t),
                 (bih_s[:], bih), (bhh_s[:], bhh), (wq_s[:], wq), (wk_s[:], wk), (wv_s[:], wv), (wo_s[:], wo),
                 (bo_s[:], bo), (gw_s[:], gat_w), (gwt_s, gat_wt), (ga_s[:], gat_a),
                 (garep_s, gat_arep), (ident_s[:], ident), (slotsum_s[:], slot_sum), (minus_s[:], minus_part)]

        @block.sync
        def _(sp):
            sp.dma_start(xnext, x[0].rearrange("(t p) d -> p t d", p=P)).then_inc(x_in, 16)
            for dst, src in loads:
                sp.dma_start(dst, src).then_inc(weights_in, 16)
            for t in range(T):
                if t >= STAGES and t % STAGES == 0:
                    sp.wait_ge(pre_done, t)
                sp.dma_start(stage[:, t % STAGES, :], adj[0, t * P:(t + 1) * P, :]).then_inc(pre_in, 16)
            sp.wait_ge(pre_done, T)
            sp.sem_inc(stored, 16)
            with sp.Fori(0, G) as g:
                sp.dma_start(mask_s[:, :], nodemask[bass.ds(g, 1)].rearrange("o p t -> p (o t)")).then_inc(S["mask_in"], 16)
                nxt = (g + 1) % G

                def load(tiles):
                    for n in tiles:
                        k, t = n % STAGES, n % T
                        if n >= STAGES:
                            sp.wait_ge(stage_used[k], n // STAGES)
                        src = (adj[bass.ds(g, 1)], adj_t[bass.ds(g, 1)], adj[bass.ds(nxt, 1)])[n // T]
                        sp.dma_start(stage[:, k, :], src[:, t * P:(t + 1) * P, :].rearrange("o p n -> (o p) n")
                                     ).then_inc(stage_in[k], 16)

                load(range(2 * T + STAGES))
                sp.wait_ge(stored, 16 * (g + 1))
                sp.sem_inc(resumed, 1)
                for heads, landed in ((slice(0, 2), "rows0_in"), (slice(2, HEADS), "rows_in")):
                    for part, ready in enumerate(("part1_ready", "part2_ready", "part3_ready")):
                        for b, (blocks, src, dst) in enumerate(((Q_BLOCKS, qp, q_rows), (K_BLOCKS, kp, k_rows))):
                            if heads.start == 0:
                                sp.wait_ge(S[ready], 2 * (b + 1))
                            for n, p in enumerate(blocks):
                                if p == part:
                                    sp.dma_start(dst[n * HD:(n + 1) * HD, heads, :], src[HD * heads.start:HD * heads.stop, part, :]
                                                 ).then_inc(S[landed], 16)
                for hp in range(PAIRS):
                    if hp == 1:
                        load(range(2 * T + STAGES, 3 * T))
                    sp.wait_ge(S["maxrow_ready"], hp + 1)
                    for p in range(PARTS):
                        sp.dma_start(q_rows[ROWS + p:ROWS + p + 1, 2 * hp:2 * hp + 2, :],
                                     maxrow[p * 2 * T:(p + 1) * 2 * T, hp % 2, :]).then_inc(max_in[hp], 16)
                sp.dma_start(xnext, x[bass.ds(nxt, 1)].rearrange("o (t p) d -> p (o t) d", p=P)).then_inc(x_in, 16)
                sp.wait_ge(S["result_ready"], 1)
                sp.wait_ge(x_in, 16 * (g + 2))
                sp.sem_inc(resumed, 1)
                sp.dma_start(out[bass.ds(g, 1)].rearrange("o (t p) d -> p (o t) d", p=P),
                             result.rearrange("p (t d) -> p t d", t=T)).then_inc(stored, 16)
                end_graph(sp, g, SP_CLEARS)
            sp.wait_ge(stored, 16 * (G + 1))

        @block.gpsimd
        def _(pool):
            filled = 0
            for dst, value in ((ones_s[:], 1.0), (vp[:, :, :, :], 0.0), (vp[:, :, :, HD:HD + 1], 1.0),
                               (k_rows[ROWS:ROWS + SLOT, :, :], -1.0), (wh[:, :, D:OW], 1.0),
                               (parts_s[:], 0.0), (parts_s[0:PARTS, :], 1.0)):
                if filled:
                    pool.wait_ge(filled_s, filled)
                pool.memset(dst, value).then_inc(filled_s, 1)
                filled += 1
            pool.wait_ge(filled_s, filled)
            pool.sem_inc(consts_ready, 1)
            pool.wait_ge(pre_done, T)
            with pool.Fori(0, G) as g:
                for n in range(2 * T):
                    k, t = n % STAGES, n % T
                    pool.wait_ge(stage_in[k], 16 * (n // STAGES + 1))
                    dst = (noedge, noedge_t)[n // T]
                    pool.tensor_scalar(dst[:, t, :], stage[:, k, :], 0.0, NO_EDGE, ALU.is_le, ALU.mult
                                       ).then_inc(stage_used[k], 1)
                end_graph(pool, g, POOL_CLEARS)

        def stage_tiles_done(eng, upto):
            for k in range(STAGES):
                eng.wait_ge(stage_used[k], (upto - k + STAGES - 1) // STAGES)

        @block.vector
        def _(dve):
            v = nc.vector

            def normalise(features, link, after):
                for t in range(T):
                    last = v.bn_stats(stats[:, t, :], features[:, t, :])
                link(last)
                for t in range(T):
                    last = v.bn_aggr(mv[:, t, :], stats[:, t, :])
                link(last)
                link(v.tensor_scalar(nt1[:], mv[:, :, 1], EPS, None, ALU.add))
                link(v.tensor_scalar(seed[:], nt1[:].bitcast(I32), 1, None, ALU.arith_shift_right))
                link(v.tensor_scalar(seed[:], seed[:], -1.0, float(0x5F3759DF), ALU.mult, ALU.add))
                y, y_next = seed[:].bitcast(F32), nt3[:]
                for _ in range(NEWTON):
                    link(v.tensor_tensor(nt2[:], y, y, ALU.mult))
                    link(v.scalar_tensor_tensor(out=nt2[:], in0=nt2[:], scalar=-0.5, in1=nt1[:],
                                                op0=ALU.mult, op1=ALU.mult))
                    link(v.scalar_tensor_tensor(out=y_next, in0=nt2[:], scalar=1.5, in1=y,
                                                op0=ALU.add, op1=ALU.mult))
                    y, y_next = y_next, y
                for t in range(T):
                    v.tensor_scalar(xn[:, t, :], features[:, t, :], mv[:, t, 0:1], y[:, t:t + 1],
                                    ALU.subtract, ALU.mult).then_inc(after, 1)

            pre_links = [0]

            def pre_link(ins):
                pre_links[0] += 1
                ins.then_inc(pre_chain, 1)
                dve.wait_ge(pre_chain, pre_links[0])

            dve.wait_ge(x_in, 16)
            normalise(xnext, pre_link, normed)

            dve.wait_ge(weights_in, 16 * len(loads))
            v.tensor_copy(identb_s[:], ident_s[:]).then_inc(consts_ready, 1)
            v.tensor_tensor(brz_s[:], bih_s[:], bhh_s[:], ALU.add).then_inc(consts_ready, 1)
            for p in range(2):
                v.tensor_scalar(minusdiag_s[:, p, :], ident_s[:], minus_s[:, p:p + 1], None, ALU.mult).then_inc(consts_ready, 1)
            dve.wait_ge(folded, 1)
            for k in range(2):
                v.tensor_copy(warep_s[:, k, :, :].rearrange("p c n -> p (c n)"), psum[:, k, 0:2 * P]).then_inc(consts_ready, 1)
                v.tensor_copy(wa_s[:, k, :], psum[:, k, 2 * P:2 * P + 2]).then_inc(consts_ready, 1)
            for t in range(T):
                if t % STAGES == 0:
                    dve.wait_ge(pre_in, 16 * (t + STAGES))
                v.tensor_scalar(edge01[:, t, :], stage[:, t % STAGES, :], 0.0, None, ALU.not_equal).then_inc(pre_done, 1)

            with dve.Fori(0, G) as g:
                links = [0]

                def link(ins):
                    links[0] += 1
                    ins.then_inc(S["chain"], 1)
                    dve.wait_ge(S["chain"], links[0])

                v.tensor_copy(xs[:, :, :], xnext).then_inc(S["x_saved"], 1)
                dve.wait_ge(S["x_saved"], 1)
                for l in range(LAYERS):
                    for h in range(2):
                        c = slice(h * HALF, (h + 1) * HALF)
                        dve.wait_ge(S["m1_ready"], 2 * l + h + 1)
                        v.tensor_tensor(res1[:, c], psum[:, h, :], m1[:, c], ALU.subtract).then_inc(S["res_ready"], 1)
                        dve.wait_ge(S["m2_ready"], 2 * l + h + 1)
                        v.tensor_tensor(m3[:, c], res1[:, c], m2[:, c], ALU.subtract).then_inc(S["m3_ready"], 1)
                    for h in range(2):
                        c = slice(h * HALF, (h + 1) * HALF)
                        dve.wait_ge(S["rT_ready"], 2 * l + h + 1)
                        dve.wait_ge(S["hn_ready"], 2 * l + h + 1)
                        link(v.scalar_tensor_tensor(out=tT[:, c], in0=psum[:, h, :], scalar=bhh_s[:, 2:3], in1=rT[:, c],
                                                    op0=ALU.add, op1=ALU.mult))
                        dve.wait_ge(S["n_ready"], 2 * l + h + 1)
                        v.tensor_tensor(tT[:, c], psum[:, 2 + h, :], tT[:, c], ALU.add).then_inc(S["t_ready"], 1)
                        dve.wait_ge(S["nT_ready"], 2 * l + h + 1)
                        link(v.tensor_tensor(tT[:, c], hT[:, c], nT[:, c], ALU.subtract))
                        dve.wait_ge(S["zT_ready"], 2 * l + h + 1)
                        link(v.tensor_tensor(tT[:, c], tT[:, c], zT[:, c], ALU.mult))
                        v.tensor_tensor(hT[:, c], tT[:, c], nT[:, c], ALU.add).then_inc(S["h_ready"], 1)
                for h in range(2):
                    dve.wait_ge(S["back_ready"], h + 1)
                    o = xs[:, h * TH:(h + 1) * TH, :].rearrange("p t d -> p (t d)")
                    last = v.tensor_tensor(o, psum[:, h, :], o, ALU.add)
                link(last)

                normalise(xs, link, S["norm_ready"])
                def rest_of(n):
                    part, c, scale = (qp, kp)[n // 2], halves[n % 2], (HD ** -0.5, 1.0)[n // 2]
                    dve.wait_ge(S["part1_ready"], n + 1)
                    v.scalar_tensor_tensor(out=workn[:, n // 2, c], in0=psum[:, n, :], scalar=scale, in1=part[:, 0, c],
                                           op0=ALU.mult, op1=ALU.subtract).then_inc(S["rest_ready"], 1)

                def third_of(n):
                    part, c = (qp, kp)[n // 2], halves[n % 2]
                    dve.wait_ge(S["part2_ready"], n + 1)
                    v.tensor_tensor(part[:, 2, c], workn[:, n // 2, c], part[:, 1, c], ALU.subtract).then_inc(S["part3_ready"], 1)

                rest_of(0)
                rest_of(1)
                for n in range(2):
                    third_of(n)
                    rest_of(n + 2)
                third_of(2)
                third_of(3)

                def empty(use):
                    n, kind = slot_at[use], use[0]
                    bank = 2 * (n % 2)
                    dve.wait_ge(S["slot_ready"], n + 1)
                    if kind == "row":
                        _, hp, t, a = use
                        v.tensor_tensor_reduce(junk[:, n % 2, :], two_banks(bank), noedge[:, t, :], 1.0, LOWEST,
                                               ALU.add, ALU.max, rowmax[:, hp, a * T + t:a * T + t + 1]
                                               ).then_inc(S["slot_free"], 1)
                    elif kind == "max":
                        hp = use[1]
                        if hp >= 2:
                            dve.wait_ge(max_in[hp - 2], 16 * PARTS)
                        v.tensor_copy(maxrow[:, hp % 2, :], psum[0:PARTS * 2 * T, bank, :].bitcast(BF16)[:, 0:P]
                                      ).then_inc(S["slot_free"], 1)
                        dve.wait_ge(S["slot_free"], n + 1)
                        dve.sem_inc(S["maxrow_ready"], 1)
                    elif kind == "sum":
                        hp = use[1]
                        if hp:
                            dve.wait_ge(S["slot_free"], slot_at[("sum", hp - 1)] + 1)
                        if hp == PAIRS - 1:
                            for c in quarters:
                                link(v.reciprocal(rl[:, c], psum[:, bank, c]))
                                v.tensor_tensor(ctxn[:, hp, c], pvs[:, hp % 2, c], rl[:, c], ALU.mult).then_inc(S["divided"], 1)
                            return
                        link(v.reciprocal(rl[:], psum[:, bank, :]))
                        v.tensor_tensor(ctxn[:, hp, :], pvs[:, hp % 2, :], rl[:], ALU.mult).then_inc(S["slot_free"], 1)
                    elif kind == "wo":
                        for h in range(2):
                            o = xs[:, h * TH:(h + 1) * TH, :].rearrange("p t d -> p (t d)")
                            last = v.tensor_tensor(o, psum[:, bank + h, :], o, ALU.add)
                        link(last)

                def cut_maxima(hp):
                    c = [maxpart[:, hp % 2, p * 2 * T:(p + 1) * 2 * T] for p in range(PARTS)]
                    rest = maxrest[:, hp % 2, :]
                    dve.wait_ge(S["slot_free"], slot_at[("row", hp, T - 1, 1)] + 1)
                    link(v.tensor_copy(c[0], rowmax[:, hp, :]))
                    link(v.tensor_tensor(rest, rowmax[:, hp, :], c[0], ALU.subtract))
                    link(v.tensor_copy(c[1], rest))
                    v.tensor_tensor(c[2], rest, c[1], ALU.subtract).then_inc(S["maxpart_ready"], 1)

                stage_tiles_done(dve, T)
                for use in slot_order[:-2]:
                    if use[0] == "max":
                        cut_maxima(use[1])
                    empty(use)
                    if use in convert_after:
                        n = 2 * T + convert_after.index(use)
                        dve.wait_ge(stage_in[n % STAGES], 16 * (n // STAGES + 1))
                        v.tensor_scalar(edge01[:, n % T, :], stage[:, n % STAGES, :], 0.0, None, ALU.not_equal
                                        ).then_inc(stage_used[n % STAGES], 1)
                xs_flat = xs[:, :, :].rearrange("p t d -> p (t d)")
                link(v.tensor_tensor(xs[:, :, :], xs[:, :, :], bo_s[:, None, :].to_broadcast([P, T, D]), ALU.add))
                empty(("sum", PAIRS - 1))
                empty(("wo",))

                for k in range(2):
                    normalise(xs, link, S["norm_ready"])
                    dve.wait_ge(S["f2_ready"], k + 1)
                    for t in range(T):
                        if t >= 2:
                            dve.wait_ge(S["chain"], links[0] - 1)
                        v.tensor_tensor_reduce(junk[:, t % 2, :], two_banks(5), noedge[:, t, :], 1.0, LOWEST,
                                               ALU.add, ALU.max, mf2[:, t:t + 1]).then_inc(S["chain"], 1)
                        links[0] += 1
                        if t == T // 2:
                            dve.wait_ge(S["fcol_ready"], k + 1)
                            v.tensor_copy(fcol[:, :, :].rearrange("p t c -> p (t c)"), psum[:, 0, 0:2 * T]).then_inc(S["fcol_saved"], 1)
                    dve.wait_ge(S["chain"], links[0])
                    dve.wait_ge(S["fcol_saved"], k + 1)
                    link(v.tensor_tensor(gx[:], mf2[:], fcol[:, :, 0], ALU.add))
                    link(v.scalar_tensor_tensor(out=gm[:], in0=gx[:], scalar=SLOPE, in1=gx[:], op0=ALU.mult, op1=ALU.max))
                    v.tensor_tensor(diag.rearrange("p (t n) -> p t n", t=T), ident_s[:, None, :].to_broadcast([P, T, P]),
                                    gm[:, :, None].to_broadcast([P, T, P]), ALU.mult).then_inc(S["diag_ready"], 1)

                    def lrelu(t):
                        dve.wait_ge(S["gsum_ready"], k * T + t + 1)
                        y = workn[:, t % YBUFS, :]
                        v.scalar_tensor_tensor(out=y, in0=y, scalar=SLOPE, in1=y, op0=ALU.mult, op1=ALU.max
                                               ).then_inc(S["lrelu_ready"], 1)

                    lrelu(0)
                    lrelu(1)
                    dve.wait_ge(S["mrow_ready"], 2 * (k + 1))
                    for t in range(T):
                        if 0 < t < T - 1:
                            lrelu(t + 1)
                        dve.wait_ge(S["lrelu_ready"], k * T + t + 1)
                        y = workn[:, t % YBUFS, :]
                        v.tensor_tensor(y, y, mrow, ALU.subtract).then_inc(S["shifted_ready"], 1)
                    if k == 1:
                        dve.wait_ge(x_in, 16 * (g + 2))
                        dve.sem_inc(resumed, 1)
                        normalise(xnext, link, normed)
                    dve.wait_ge(S["gpv_step"], T * (k + 1))
                    for b in range(3):
                        nb = min(3, T - 3 * b)
                        o = psum[:, 5 + b, 0:nb * OW].rearrange("p (t c) -> p t c", c=OW)
                        last = v.reciprocal(rinv[:, 3 * b:3 * b + nb], o[:, :, D])
                    link(last)
                    if k == 0:
                        dve.wait_ge(S["mask_in"], 16)
                        link(v.tensor_tensor(rinv[:], rinv[:], mask_s[:], ALU.mult))
                    up = gup.rearrange("p (t d) -> p t d", t=T)
                    for b in range(3):
                        nb = min(3, T - 3 * b)
                        o = psum[:, 5 + b, 0:nb * OW].rearrange("p (t c) -> p t c", c=OW)
                        last = v.tensor_tensor(up[:, 3 * b:3 * b + nb, :], o[:, :, 0:D],
                                               rinv[:, 3 * b:3 * b + nb, None].to_broadcast([P, nb, D]), ALU.mult)
                    last.then_inc(S["gout_ready"], 1)
                    dve.wait_ge(S["gout_ready"], k + 1)
                    if k == 0:
                        v.tensor_scalar(gmin, gup, 0.0, None, ALU.min).then_inc(S["elu_in"], 1)
                        link(v.scalar_tensor_tensor(out=xs_flat, in0=gup, scalar=0.0, in1=xs_flat, op0=ALU.max, op1=ALU.add))
                        dve.wait_ge(S["elu_out"], 1)
                        link(v.scalar_tensor_tensor(out=xs_flat, in0=gexp, scalar=-1.0, in1=xs_flat, op0=ALU.add, op1=ALU.add))
                    else:
                        v.scalar_tensor_tensor(out=result, in0=gup, scalar=0.0, in1=xs_flat, op0=ALU.max, op1=ALU.add
                                               ).then_inc(S["result_ready"], 1)
                end_graph(dve, g, DVE_CLEARS)

        @block.scalar
        def _(act):
            a = nc.scalar

            def turn_in(k):
                for h in range(2):
                    act.wait_ge(S["turned"], 2 * k + h + 1)
                    a.activation(hT[:, h * HALF:(h + 1) * HALF], psum[:, h, :], ACT.Relu).then_inc(S["hT_ready"], 1)

            act.wait_ge(consts_ready, CONSTS)
            with act.Fori(0, G) as g:
                turn_in(0)
                act.wait_ge(S["x_saved"], 1)
                for l in range(LAYERS):
                    for h in range(2):
                        c = slice(h * HALF, (h + 1) * HALF)
                        act.wait_ge(S["msg_ready"], 2 * l + h + 1)
                        a.copy(m1[:, c], psum[:, h, :]).then_inc(S["m1_ready"], 1)
                        act.wait_ge(S["res_ready"], 2 * l + h + 1)
                        a.copy(m2[:, c], res1[:, c]).then_inc(S["m2_ready"], 1)
                    for h in range(2):
                        c = slice(h * HALF, (h + 1) * HALF)
                        act.wait_ge(S["agg_ready"], 2 * l + h + 1)
                        a.copy(aggT[:, c], psum[:, 2 + h, :]).then_inc(S["aggT_ready"], 1)
                    for h in range(2):
                        c = slice(h * HALF, (h + 1) * HALF)
                        act.wait_ge(S["r_ready"], 2 * l + h + 1)
                        a.activation(rT[:, c], psum[:, 4 + h, :], ACT.Sigmoid, bias=brz_s[:, 0:1]).then_inc(S["rT_ready"], 1)
                        act.wait_ge(S["z_ready"], 2 * l + h + 1)
                        a.activation(zT[:, c], psum[:, 6 + h, :], ACT.Sigmoid, bias=brz_s[:, 1:2]).then_inc(S["zT_ready"], 1)
                        act.wait_ge(S["t_ready"], 2 * l + h + 1)
                        a.activation(nT[:, c], tT[:, c], ACT.Tanh, bias=bih_s[:, 2:3]).then_inc(S["nT_ready"], 1)

                turn_in(1)
                def first_of(n):
                    act.wait_ge(S["proj_ready"], n + 1)
                    a.activation((qp, kp)[n // 2][:, 0, halves[n % 2]], psum[:, n, :], ACT.Copy,
                                 scale=(HD ** -0.5, 1.0)[n // 2]).then_inc(S["part1_ready"], 1)

                def second_of(n):
                    act.wait_ge(S["rest_ready"], n + 1)
                    a.copy((qp, kp)[n // 2][:, 1, halves[n % 2]], workn[:, n // 2, halves[n % 2]]).then_inc(S["part2_ready"], 1)

                first_of(0)
                first_of(1)
                for n in range(2):
                    second_of(n)
                    first_of(n + 2)
                second_of(2)
                second_of(3)
                act.wait_ge(S["v_psum"], 2)
                a.copy(vp[:, :, :, 0:HD], two_banks(4).rearrange("p (t h d) -> p t h d", t=T, h=HEADS)).then_inc(S["v_ready"], 1)
                for hp in range(PAIRS):
                    for u in range(4 * T):
                        n = 4 * T * hp + u
                        act.wait_ge(S["score_ready"], n + 1)
                        if n >= PROBS:
                            act.wait_ge(S["pv_done"], (n - PROBS) // 4 + 1)
                        a.activation(work[:, n % PROBS, :], psum[:, 4 + n % 3, :], ACT.Exp).then_inc(S["prob_ready"], 1)
                        if hp >= 1 and u == 3:
                            act.wait_ge(S["pv_done"], T * hp)
                            if hp >= 3:
                                act.wait_ge(S["slot_free"], slot_at[("sum", hp - 3)] + 1)
                            a.copy(pvs[:, (hp - 1) % 2, :], psum[:, 7, :]).then_inc(S["pair_saved"], 1)
                act.wait_ge(S["pv_done"], T * PAIRS)
                act.wait_ge(S["slot_free"], slot_at[("sum", PAIRS - 3)] + 1)
                a.copy(pvs[:, (PAIRS - 1) % 2, :], psum[:, 7, :]).then_inc(S["pair_saved"], 1)

                for k in range(2):
                    turn_in(2 + k)
                    for p in range(PARTS - 1):
                        for h in range(2):
                            act.wait_ge(S["f1_psum"], 2 * (PARTS * k + p) + h + 1)
                            a.copy(f1part[:, p, h * HALF:(h + 1) * HALF], psum[:, (4, 7)[h], :]).then_inc(S["f1_part"], 1)
                    for h in range(2):
                        act.wait_ge(S["wh_psum"], 2 * k + h + 1)
                        a.copy(wh[:, h * TH:(h + 1) * TH, 0:D],
                               psum[:, 2 + h, :].rearrange("p (t d) -> p t d", d=D)).then_inc(S["wh_ready"], 1)
                    for h in range(2):
                        act.wait_ge(S["f1_psum"], 2 * (PARTS * k + PARTS - 1) + h + 1)
                        a.copy(f1row[:, h * HALF:(h + 1) * HALF], psum[:, (4, 7)[h], :]).then_inc(S["f1_ready"], 1)

                    def add_f2(t):
                        act.wait_ge(S["gscore_ready"], k * T + t + 1)
                        act.wait_ge(S["fcol_saved"], k + 1)
                        if t >= YBUFS:
                            act.wait_ge(S["gprob_ready"], k * T + t - YBUFS + 1)
                        a.activation(workn[:, t % YBUFS, :], two_banks(1 + 2 * (t % 2)), ACT.Identity,
                                     bias=fcol[:, t, 1:2]).then_inc(S["gsum_ready"], 1)

                    add_f2(0)
                    add_f2(1)
                    for h in range(2):
                        act.wait_ge(S["mrow_psum"], 2 * k + h + 1)
                        a.copy(mrow[:, h * HALF:(h + 1) * HALF], psum[:, (0, 7)[h], :]).then_inc(S["mrow_ready"], 1)
                    add_f2(2)
                    for t in range(T):
                        act.wait_ge(S["shifted_ready"], k * T + t + 1)
                        if t >= GBUFS:
                            act.wait_ge(S["gpv_step"], k * T + t - GBUFS + 1)
                        a.activation(workn[:, YBUFS + t % GBUFS, :], workn[:, t % YBUFS, :], ACT.Exp).then_inc(S["gprob_ready"], 1)
                        if t + 3 < T:
                            add_f2(t + 3)
                    if k == 0:
                        act.wait_ge(S["elu_in"], 1)
                        a.activation(gexp, gmin, ACT.Exp).then_inc(S["elu_out"], 1)
                end_graph(act, g, ACT_CLEARS)

        @block.tensor
        def _(pe):
            mm = nc.tensor.matmul

            def turn_out(k):
                for h in range(2):
                    for t in range(TH):
                        if k:
                            pe.wait_ge(S["norm_ready"], (k - 1) * T + h * TH + t + 1)
                        last = nc.tensor.transpose(psum[:, h, t * P:(t + 1) * P], xn[:, h * TH + t, :], ident_s[:])
                    last.then_inc(S["turned"], 1)

            pe.wait_ge(weights_in, 16 * len(loads))
            for k in range(2):
                mm(psum[:, k, 0:2 * P], gwt_s[:, k, :], garep_s[:, k, :, :].rearrange("p c n -> p (c n)"), start=True, stop=True)
                last = mm(psum[:, k, 2 * P:2 * P + 2], gwt_s[:, k, :], ga_s[:, k, :], start=True, stop=True)
            last.then_inc(folded, 1)
            pe.wait_ge(consts_ready, CONSTS)
            pe.wait_ge(pre_done, T)
            pe.wait_ge(normed, T)
            with pe.Fori(0, G) as g:
                turn_out(0)
                for l in range(LAYERS):
                    def messages(h):
                        if l == 0:
                            pe.wait_ge(S["hT_ready"], h + 1)
                        else:
                            pe.wait_ge(S["h_ready"], 2 * (l - 1) + h + 1)
                        for t in range(TH):
                            last = mm(psum[:, h, t * P:(t + 1) * P], hT[:, (h * TH + t) * P:(h * TH + t + 1) * P],
                                      w0_s[:, l, :], start=True, stop=True)
                        last.then_inc(S["msg_ready"], 1)
                        for gate in range(2):
                            mm(psum[:, 4 + 2 * gate + h, :], whh_s[:, gate * D:(gate + 1) * D],
                               hT[:, h * HALF:(h + 1) * HALF], start=True, stop=False)

                    def aggregate(sh, targets):
                        for part, (m, ready) in enumerate(((m1, "m1_ready"), (m2, "m2_ready"), (m3, "m3_ready"))):
                            pe.wait_ge(S[ready], 2 * l + sh + 1)
                            for s in range(sh * TH, (sh + 1) * TH):
                                for h in targets:
                                    last = mm(psum[:, 2 + h, :], m[:, s * P:(s + 1) * P], edge01[:, s, h * HALF:(h + 1) * HALF],
                                              start=(part == 0 and s == 0), stop=(part == PARTS - 1 and s == T - 1))
                        return last

                    messages(0)
                    aggregate(0, (0, 1))
                    messages(1)
                    aggregate(1, (0,)).then_inc(S["agg_ready"], 1)
                    aggregate(1, (1,)).then_inc(S["agg_ready"], 1)
                    for h in range(2):
                        c = slice(h * HALF, (h + 1) * HALF)
                        pe.wait_ge(S["res_ready"], 2 * l + h + 1)
                        mm(psum[:, h, :], whh_s[:, 2 * D:3 * D], hT[:, c], start=True, stop=True).then_inc(S["hn_ready"], 1)
                        pe.wait_ge(S["aggT_ready"], 2 * l + h + 1)
                        mm(psum[:, 4 + h, :], wih_s[:, 0:D], aggT[:, c], start=False, stop=True).then_inc(S["r_ready"], 1)
                        mm(psum[:, 2 + h, :], wih_s[:, 2 * D:3 * D], aggT[:, c], start=True, stop=True).then_inc(S["n_ready"], 1)
                        mm(psum[:, 6 + h, :], wih_s[:, D:2 * D], aggT[:, c], start=False, stop=True).then_inc(S["z_ready"], 1)
                for h in range(2):
                    pe.wait_ge(S["h_ready"], 2 * (LAYERS - 1) + h + 1)
                    for t in range(TH):
                        last = nc.tensor.transpose(psum[:, h, t * P:(t + 1) * P],
                                                   hT[:, (h * TH + t) * P:(h * TH + t + 1) * P], ident_s[:])
                    last.then_inc(S["back_ready"], 1)

                turn_out(1)
                def fill(use):
                    n, kind = slot_at[use], use[0]
                    bank = 2 * (n % 2)
                    if n >= 2:
                        pe.wait_ge(S["slot_free"], n - 1)
                    if kind == "row":
                        _, hp, t, a = use
                        for h in range(2):
                            last = mm(psum[:, bank + h, :], q_rows[0:ROWS, 2 * hp + a, t * P:(t + 1) * P],
                                      k_rows[0:ROWS, 2 * hp + a, h * HALF:(h + 1) * HALF], start=True, stop=True)
                    elif kind == "max":
                        pe.wait_ge(S["maxpart_ready"], use[1] + 1)
                        last = nc.tensor.transpose(psum[0:PARTS * 2 * T, bank, :].bitcast(BF16)[:, 0:P],
                                                   maxpart[:, use[1] % 2, :], identb_s[:])
                    elif kind == "sum":
                        pe.wait_ge(S["pair_saved"], use[1] + 1)
                        last = mm(psum[:, bank, :], slotsum_s[:], pvs[:, use[1] % 2, :], start=True, stop=True)
                    elif kind == "wo":
                        for q in range(2):
                            pe.wait_ge(S["divided"], q + 1)
                            last = project(PAIRS - 1, (q * TH // 2 + i for i in (0, TH, 1, TH + 1)))
                    last.then_inc(S["slot_ready"], 1)

                def project(hp, tiles):
                    bank = 2 * (slot_at[("wo",)] % 2)
                    for t in tiles:
                        c = slice(t % TH * P, (t % TH + 1) * P)
                        last = mm(psum[:, bank + t // TH, c], ctxn[:, hp, c], wo_s[:, hp, t // TH, :],
                                  start=(hp == 0 and t % TH == 0), stop=(hp == PAIRS - 1), skip_group_check=True)
                    return last

                def values():
                    for h in range(2):
                        for t in range(TH):
                            last = mm(psum[:, 4 + h, t * P:(t + 1) * P], hT[:, (h * TH + t) * P:(h * TH + t + 1) * P],
                                      wv_s[:], start=True, stop=True)
                        last.then_inc(S["v_psum"], 1)

                def scores(hp, kt, js):
                    for j in js:
                        n = 4 * (T * hp + kt) + j
                        if n >= 3:
                            pe.wait_ge(S["prob_ready"], n - 2)
                        mm(psum[:, 4 + n % 3, :], identb_s[:], noedge_t[:, kt, (j % 2) * HALF:(j % 2 + 1) * HALF],
                           start=True, stop=False)
                        mm(psum[:, 4 + n % 3, :], k_rows[0:ROWS + PARTS, 2 * hp + j // 2, kt * P:(kt + 1) * P],
                           q_rows[0:ROWS + PARTS, 2 * hp + j // 2, (j % 2) * HALF:(j % 2 + 1) * HALF],
                           start=False, stop=True).then_inc(S["score_ready"], 1)

                def context(hp, kt):
                    n = T * hp + kt
                    pe.wait_ge(S["prob_ready"], 4 * n + 4)
                    if kt == 0 and hp >= 1:
                        pe.wait_ge(S["pair_saved"], hp)
                    for j in range(4):
                        last = mm(psum[SLOT * j:SLOT * (j + 1), 7, :], vp[:, kt, 2 * hp + j // 2, :],
                                  work[:, (4 * n + j) % PROBS, :], start=(kt == 0), stop=(kt == T - 1))
                    last.then_inc(S["pv_done"], 1)

                for b, w in enumerate((wq_s, wk_s)):
                    for h in range(2):
                        if b == 0:
                            pe.wait_ge(S["hT_ready"], 2 + h + 1)
                        mm(psum[:, 2 * b + h, :], w[:], hT[:, h * HALF:(h + 1) * HALF], start=True, stop=True
                           ).then_inc(S["proj_ready"], 1)
                values()
                pe.wait_ge(S["rest_ready"], 4)
                pe.wait_ge(S["rows0_in"], 16 * (len(Q_BLOCKS) + len(K_BLOCKS)))
                for use in row_uses(0):
                    fill(use)
                pe.wait_ge(S["v_ready"], 1)
                pe.wait_ge(S["rows_in"], 16 * (len(Q_BLOCKS) + len(K_BLOCKS)))
                stage_tiles_done(pe, 2 * T)
                for hp in range(PAIRS):
                    rows = [u for u in pair_uses[hp] if u[0] == "row"]
                    rest = [u for u in pair_uses[hp] if u[0] != "row"]

                    def row():
                        if rows:
                            fill(rows.pop(0))

                    for _ in range(2):
                        row()
                    pe.wait_ge(max_in[hp], 16 * PARTS)
                    for kt in range(T):
                        scores(hp, kt, (0, 1))
                        row()
                        scores(hp, kt, (2, 3))
                        row()
                        if kt:
                            context(hp, kt - 1)
                        if hp == PAIRS - 1 and kt == T // 2:
                            pe.wait_ge(S["slot_free"], slot_at[("wo",)] - 1)
                            for done in range(PAIRS - 1):
                                project(done, range(T))
                        if rest and not rows and kt >= (T - 2 if hp + 1 < PAIRS else 2):
                            fill(rest.pop(0))
                        row()
                    context(hp, T - 1)
                    for use in rest:
                        fill(use)
                fill(("sum", PAIRS - 1))
                fill(("wo",))

                for k in range(2):
                    turn_out(2 + k)
                    for h in range(2):
                        pe.wait_ge(S["hT_ready"], 2 * (2 + k) + h + 1)
                        last = mm(psum[:, 5 + h, :], warep_s[:, k, 1, :], hT[:, h * HALF:(h + 1) * HALF], start=True, stop=True)
                    last.then_inc(S["f2_ready"], 1)
                    for h in range(2):
                        mm(psum[:, (4, 7)[h], :], warep_s[:, k, 0, :], hT[:, h * HALF:(h + 1) * HALF],
                           start=True, stop=True, skip_group_check=True).then_inc(S["f1_psum"], 1)
                    for h in range(2):
                        for t in range(TH):
                            last = mm(psum[:, 2 + h, t * P:(t + 1) * P], hT[:, (h * TH + t) * P:(h * TH + t + 1) * P],
                                      gw_s[:, k, :], start=True, stop=True)
                        last.then_inc(S["wh_psum"], 1)


                    def less_part(p):
                        for h in range(2):
                            pe.wait_ge(S["f1_part"], 2 * ((PARTS - 1) * k + p) + h + 1)
                            mm(psum[:, (4, 7)[h], :], minusdiag_s[:, p, :], f1part[:, p, h * HALF:(h + 1) * HALF],
                               start=False, stop=True, skip_group_check=True).then_inc(S["f1_psum"], 1)

                    less_part(0)
                    for t in range(T):
                        last = mm(psum[:, 0, 2 * t:2 * t + 2], hT[:, t * P:(t + 1) * P], wa_s[:, k, :], start=True, stop=True)
                    last.then_inc(S["fcol_ready"], 1)
                    less_part(1)
                    pe.wait_ge(S["wh_ready"], 2 * (k + 1))
                    pe.wait_ge(S["f1_ready"], 2 * (k + 1))

                    def gat_scores(t):
                        if t >= 2:
                            pe.wait_ge(S["gsum_ready"], k * T + t - 1)
                        b = 1 + 2 * (t % 2)
                        for h in range(2):
                            mm(psum[:, b + h, :], identb_s[:], noedge_t[:, t, h * HALF:(h + 1) * HALF],
                               start=True, stop=False)
                        for h in range(2):
                            last = mm(psum[:, b + h, :], parts_s[:], f1row[:, h * HALF:(h + 1) * HALF],
                                      start=False, stop=True)
                        last.then_inc(S["gscore_ready"], 1)

                    gat_scores(0)
                    gat_scores(1)
                    pe.wait_ge(S["diag_ready"], k + 1)
                    pe.wait_ge(S["fcol_saved"], k + 1)
                    for h in range(2):
                        mm(psum[:, (0, 7)[h], :], ones_s[:], diag[:, h * HALF:(h + 1) * HALF],
                           start=True, stop=True).then_inc(S["mrow_psum"], 1)
                    gat_scores(2)
                    pe.wait_ge(S["mrow_ready"], 2 * (k + 1))
                    for t in range(T):
                        if t + 3 < T:
                            gat_scores(t + 3)
                        pe.wait_ge(S["gprob_ready"], k * T + t + 1)
                        for i in range(T):
                            last = mm(psum[:, 5 + i // 3, (i % 3) * OW:(i % 3) * OW + D + 1],
                                      workn[:, YBUFS + t % GBUFS, i * P:(i + 1) * P], wh[:, t, 0:D + 1],
                                      start=(t == 0 and i % 3 == 0), stop=(t == T - 1), skip_group_check=True)
                        last.then_inc(S["gpv_step"], 1)
                end_graph(pe, g, PE_CLEARS)


def kernel(x, adj, nodemask, L0_gnn_weight, L0_gnn_w_ih, L0_gnn_w_hh, L0_gnn_b_ih, L0_gnn_b_hh,
           L1_gnn_Wq, L1_gnn_Wk, L1_gnn_Wv, L1_gnn_Wo, L1_gnn_bo, L2_gnn_W, L2_gnn_a, L3_gnn_W, L3_gnn_a):
    import numpy as np
    import concourse.bacc as bacc
    from concourse.bass_utils import run_bass_kernel_spmd as run

    def by_row(w):
        heads = w.reshape(D, HEADS, HD).transpose(0, 2, 1)
        return np.concatenate([heads[:, :, :2].reshape(D, 2 * HD), heads[:, :, 2:].reshape(D, D - 2 * HD)], axis=1)

    def pair_rows(w):
        o = np.zeros((PAIRS, 2, 2, 2, SLOT, D), w.dtype)
        rows = w.reshape(PAIRS, 2, HD, D)
        for b in range(2):
            o[:, b, :, b, :HD] = rows
        return o.reshape(PAIRS, 2, P, D).transpose(2, 0, 1, 3)

    f32 = np.float32
    row = np.arange(P)
    minus_part = -np.stack([(row >= 1) & (row < PARTS), row == PARTS - 1], axis=1).astype(f32)
    slot_sum = ((row[:, None] % SLOT == HD) & (row[:, None] // SLOT == row[None, :] // SLOT)).astype(f32)
    x, adj, nodemask = np.asarray(x), np.asarray(adj), np.asarray(nodemask)
    gat_a = [np.asarray(a).reshape(2, D) for a in (L2_gnn_a, L3_gnn_a)]
    arrays = {
        "x": x, "adj": adj, "adj_t": adj.transpose(0, 2, 1),
        "nodemask": nodemask.reshape(G, T, P).transpose(0, 2, 1),
        "w0": np.asarray(L0_gnn_weight), "wih_t": np.asarray(L0_gnn_w_ih).T, "whh_t": np.asarray(L0_gnn_w_hh).T,
        "bih": np.asarray(L0_gnn_b_ih).reshape(3, D).T, "bhh": np.asarray(L0_gnn_b_hh).reshape(3, D).T,
        "wq": by_row(np.asarray(L1_gnn_Wq)), "wk": by_row(np.asarray(L1_gnn_Wk)),
        "wv": np.asarray(L1_gnn_Wv), "wo": pair_rows(np.asarray(L1_gnn_Wo)),
        "bo": np.repeat(np.asarray(L1_gnn_bo)[None, :], P, axis=0),
        "gat_w": np.stack([np.asarray(L2_gnn_W), np.asarray(L3_gnn_W)], axis=1),
        "gat_wt": np.stack([np.asarray(L2_gnn_W).T, np.asarray(L3_gnn_W).T], axis=1),
        "gat_a": np.stack([a.T for a in gat_a], axis=1),
        "gat_arep": np.repeat(np.stack([a.T for a in gat_a], axis=1)[..., None], P, axis=3),
        "ident": np.eye(P, dtype=f32), "slot_sum": slot_sum, "minus_part": minus_part,
    }
    nc = bacc.Bacc("TRN2", target_bir_lowering=False, num_devices=1)
    feed, args = {}, []
    for name, a in arrays.items():
        feed["in_" + name] = np.ascontiguousarray(a)
        args.append(nc.dram_tensor("in_" + name, a.shape, mybir.dt.from_np(a.dtype), kind="ExternalInput").ap())
    out = nc.dram_tensor("out", (G, N, D), F32, kind="ExternalOutput").ap()
    build(nc, *args, out)
    return run(nc, [feed], core_ids=[0]).results[0]["out"]
```
